# Optimizing a Trainium2 kernel written in Bass

```python
import numpy as np
import jax
import jax.numpy as jnp

def _softmax(x, axis=-1):
    return jax.nn.softmax(x, axis=axis)
def _gelu(x):
    return jax.nn.gelu(x, approximate=True)
def _silu(x):
    return jax.nn.silu(x)
def _sigmoid(x):
    return jax.nn.sigmoid(x)
def _layernorm(x, axis=-1, eps=1e-5):
    m = jnp.mean(x, axis=axis, keepdims=True)
    v = jnp.var(x, axis=axis, keepdims=True)
    return (x - m) / jnp.sqrt(v + eps)
def _scatter_add(tgt, idx, src, axis=0):
    return tgt.at[idx].add(src)
def _segment_sum(src, seg, n):
    return jax.ops.segment_sum(src, seg, n)

kernel_name = 'mk_conv_attn_hybrid_d2_conv_nhwc128_e7f0a8'

def setup_inputs(seed: int = 0):
    np.random.seed(seed)
    _w = jnp.asarray
    def _rec_inputs():
        import jax
        import jax.numpy as jnp
        _gk = jax.random.key(seed)
        x = -0.0005207 + 1.001 * jax.random.normal(jax.random.fold_in(_gk, 1), (4, 64, 64, 128), jnp.float32)
        return x
    x = _rec_inputs()
    def _L0_conv_setup():
        import jax, jax.numpy as jnp
        import numpy as np
        HEADS = 4
        DIM_HEAD = 32
        SCALE = 10.0
        EPS = 1e-12

        def l2norm_axis1(t):
            denom = jnp.clip(jnp.linalg.norm(t, ord=2, axis=1, keepdims=True), EPS)
            return t / denom
        key = jax.random.key(seed)
        k1, k2, k3 = jax.random.split(key, 3)
        B, H, W, C = (4, 64, 64, 128)
        dim = HEADS * DIM_HEAD
        x = jax.random.normal(k1, (B, H, W, C), dtype=jnp.float32)
        w_qkv = jax.random.normal(k2, (C, dim * 3), dtype=jnp.float32) * (1.0 / np.sqrt(C))
        w_out = jax.random.normal(k3, (dim, C), dtype=jnp.float32) * (1.0 / np.sqrt(dim))
        b_out = jnp.zeros((C,), dtype=jnp.float32)
        return {'x': x, 'w_qkv': w_qkv, 'w_out': w_out, 'b_out': b_out}
    _L0_conv_all = _L0_conv_setup()
    _L0_conv_in = {k: v for k, v in _L0_conv_all.items() if k in ('w_qkv', 'w_out', 'b_out', )}
    del _L0_conv_all

    def _L1_attn_setup():
        import jax, jax.numpy as jnp
        import numpy as np
        B, L, C, H = (8, 16384, 128, 4)
        EPS = 1e-05
        key = jax.random.key(seed)
        k1, k2, k3, k4 = jax.random.split(key, 4)
        return {'x': jax.random.normal(k1, (B, L, C), dtype=jnp.float32), 'W_qkv': jax.random.normal(k2, (3 * C, C), dtype=jnp.float32) * C ** (-0.5), 'W_out': jax.random.normal(k3, (C, C), dtype=jnp.float32) * C ** (-0.5), 'b_out': jax.random.normal(k4, (C,), dtype=jnp.float32) * 0.01, 'gn_w': jnp.ones((C,), dtype=jnp.float32), 'gn_b': jnp.zeros((C,), dtype=jnp.float32)}
    _L1_attn_all = _L1_attn_setup()
    _L1_attn_in = {k: v for k, v in _L1_attn_all.items() if k in ('W_qkv', 'W_out', 'b_out', 'gn_w', 'gn_b', )}
    del _L1_attn_all

    def _L1_ffn_setup():
        import jax, jax.numpy as jnp
        import numpy as np
        B, N, D, C, E, K = (8, 8192, 128, 128, 8, 2)
        key = jax.random.key(seed)
        k0, k1, k2 = jax.random.split(key, 3)
        x = jax.random.normal(k0, (B, N, D), dtype=jnp.float32)
        router_w = jax.random.normal(k1, (D, E), dtype=jnp.float32) * 0.05
        router_b = jnp.zeros((E,), dtype=jnp.float32)
        expert_w = jax.random.normal(k2, (E, D, C), dtype=jnp.float32) * (1.0 / np.sqrt(D))
        expert_b = jnp.zeros((E, C), dtype=jnp.float32)
        return {'x': x, 'router_w': router_w, 'router_b': router_b, 'expert_w': expert_w, 'expert_b': expert_b}
    _L1_ffn_all = _L1_ffn_setup()
    _L1_ffn_in = {k: v for k, v in _L1_ffn_all.items() if k in ('router_w', 'router_b', 'expert_w', 'expert_b', )}
    del _L1_ffn_all

    return {
        "x": x,
        "L0_conv_w_qkv": _L0_conv_in["w_qkv"],
        "L0_conv_w_out": _L0_conv_in["w_out"],
        "L0_conv_b_out": _L0_conv_in["b_out"],
        "L1_attn_W_qkv": _L1_attn_in["W_qkv"],
        "L1_attn_W_out": _L1_attn_in["W_out"],
        "L1_attn_b_out": _L1_attn_in["b_out"],
        "L1_attn_gn_w": _L1_attn_in["gn_w"],
        "L1_attn_gn_b": _L1_attn_in["gn_b"],
        "L1_ffn_router_w": _L1_ffn_in["router_w"],
        "L1_ffn_router_b": _L1_ffn_in["router_b"],
        "L1_ffn_expert_w": _L1_ffn_in["expert_w"],
        "L1_ffn_expert_b": _L1_ffn_in["expert_b"],
    }

def reference(x, L0_conv_w_qkv, L0_conv_w_out, L0_conv_b_out, L1_attn_W_qkv, L1_attn_W_out, L1_attn_b_out, L1_attn_gn_w, L1_attn_gn_b, L1_ffn_router_w, L1_ffn_router_b, L1_ffn_expert_w, L1_ffn_expert_b):
    import jax
    import jax.numpy as jnp
    def _L0_conv_ref(x, w_qkv, w_out, b_out):
        import jax, jax.numpy as jnp
        import numpy as np
        HEADS = 4
        DIM_HEAD = 32
        SCALE = 10.0
        EPS = 1e-12

        def l2norm_axis1(t):
            denom = jnp.clip(jnp.linalg.norm(t, ord=2, axis=1, keepdims=True), EPS)
            return t / denom
        B, H, W, C = x.shape
        dim = HEADS * DIM_HEAD
        qkv = jnp.einsum('bxyc,cf->bxyf', x, w_qkv)
        q, k, v = jnp.split(qkv, 3, axis=-1)

        def to_seq(t):
            return t.reshape(B, H * W, HEADS, DIM_HEAD)
        q, k, v = (to_seq(q), to_seq(k), to_seq(v))
        q = l2norm_axis1(q)
        k = l2norm_axis1(k)
        sim = jnp.einsum('bihd,bjhd->bhij', q, k) * SCALE
        attn = jax.nn.softmax(sim, axis=-1)
        out = jnp.einsum('bhij,bjhd->bhid', attn, v)
        out = out.transpose(0, 2, 1, 3).reshape(B, H, W, dim)
        out = jnp.einsum('bxyd,dc->bxyc', out, w_out) + b_out
        return out

    def _L1_attn_ref(x, W_qkv, W_out, b_out, gn_w, gn_b):
        import jax, jax.numpy as jnp
        import numpy as np
        B, L, C, H = (8, 16384, 128, 4)
        EPS = 1e-05
        b, l, c = x.shape
        h = H
        d = c // h
        scale = d ** (-0.5)
        xc = jnp.swapaxes(x, 1, 2)
        qkv = jnp.einsum('oc,bcl->bol', W_qkv, xc)
        q, k, v = jnp.split(qkv, 3, axis=1)
        q = q.reshape(b, h, d, l)
        k = k.reshape(b, h, d, l)
        v = v.reshape(b, h, d, l)
        q = jax.nn.softmax(q, axis=2) * scale
        k = jax.nn.softmax(k, axis=3)
        context = jnp.einsum('bhcj,bhdj->bhcd', k, v)
        out = jnp.einsum('bhcd,bhdi->bhci', context, q)
        out = out.reshape(b, h * d, l)
        out = jnp.einsum('oc,bcl->bol', W_out, out) + b_out[None, :, None]
        mean = jnp.mean(out, axis=(1, 2), keepdims=True)
        var = jnp.var(out, axis=(1, 2), keepdims=True)
        out = (out - mean) * jax.lax.rsqrt(var + EPS)
        out = out * gn_w[None, :, None] + gn_b[None, :, None]
        return jnp.swapaxes(out, 1, 2)

    def _L1_ffn_ref(x, router_w, router_b, expert_w, expert_b):
        import jax, jax.numpy as jnp
        import numpy as np
        B, N, D, C, E, K = (8, 8192, 128, 128, 8, 2)
        router_probs = jax.nn.softmax(x @ router_w + router_b, axis=-1)
        top_p, top_i = jax.lax.top_k(router_probs, K)
        top_p = top_p / jnp.sum(top_p, axis=-1, keepdims=True)
        expert_out = jnp.einsum('bnd,edc->bnec', x, expert_w) + expert_b
        gathered = jnp.take_along_axis(expert_out, top_i[..., None], axis=2)
        return jnp.einsum('bnk,bnkc->bnc', top_p, gathered)

    def _gn(v, G=32, eps=1e-5):
        B_, H_, W_, C_ = v.shape
        g = v.reshape(B_, H_, W_, G, C_ // G)
        m = jnp.mean(g, axis=(1, 2, 4), keepdims=True)
        s = jnp.var(g, axis=(1, 2, 4), keepdims=True)
        return ((g - m) / jnp.sqrt(s + eps)).reshape(v.shape)

    def _ln_c(v, eps=1e-6):
        m = jnp.mean(v, axis=-1, keepdims=True)
        s = jnp.var(v, axis=-1, keepdims=True)
        return (v - m) / jnp.sqrt(s + eps)

    def _ln_t(v, eps=1e-5):
        m = jnp.mean(v, axis=-1, keepdims=True)
        s = jnp.var(v, axis=-1, keepdims=True)
        return (v - m) / jnp.sqrt(s + eps)

    def _to_tokens(v):
        B_, H_, W_, C_ = v.shape
        return v.reshape(B_, H_ * W_, C_)
    def _from_tokens(t, like):
        return t.reshape(like.shape)

    x = x + _L0_conv_ref(_gn(x), L0_conv_w_qkv, L0_conv_w_out, L0_conv_b_out)
    t = _to_tokens(x)
    t = t + _L1_attn_ref(_ln_t(t), L1_attn_W_qkv, L1_attn_W_out, L1_attn_b_out, L1_attn_gn_w, L1_attn_gn_b)
    t = t + _L1_ffn_ref(_ln_t(t), L1_ffn_router_w, L1_ffn_router_b, L1_ffn_expert_w, L1_ffn_expert_b)
    x = _from_tokens(t, x)
    return x


_drawn_inputs = setup_inputs


def setup_inputs(seed=0):
    import zlib

    import numpy as np

    out = dict(_drawn_inputs(seed))
    spreads = {'L0_conv_b_out': (0.0, 0.1),
     'L1_attn_gn_w': (1.0, 0.2),
     'L1_attn_gn_b': (0.0, 0.1),
     'L1_ffn_router_b': (0.0, 0.1),
     'L1_ffn_expert_b': (0.0, 0.1)}
    factors = {}
    for name, (base, spread) in spreads.items():
        noise = np.random.default_rng([zlib.crc32(name.encode()), seed]).standard_normal(out[name].shape)
        drawn = base * np.exp(spread * noise) if base else spread * noise
        out[name] = jnp.asarray(drawn.astype(out[name].dtype))
    for name, factor in factors.items():
        out[name] = (out[name] * factor).astype(out[name].dtype)
    return out
```

```python
import numpy as np
import concourse.bass as bass
from concourse import mybir
from contextlib import ExitStack

F32 = mybir.dt.float32
F32R = mybir.dt.float32r
U32 = mybir.dt.uint32
I32 = mybir.dt.int32
ALU = mybir.AluOpType
ACT = mybir.ActivationFunctionType
X_AX = mybir.AxisListType.X

P = 128
B = 4
N = 64 * 64
C = 128
T = N // P
H = 4
D = C // H
CH = 512
NCH = N // CH
TPB = CH // P
G = 32
EXPERTS = 8
SCALE0 = 10.0
SCALE1 = D ** -0.5
SAFE_BOUND = 40.0
MAGIC = 0x5F3759DF

STEPS = 2 * T
AHEAD = 3
SCORED = STEPS * NCH + AHEAD
RING = 8
GROUP = 4
NG = T // GROUP
ADDS = 2 * (GROUP - 1)
QLOADS = (NCH + 1) * 16 * 4 * H
GEN = STEPS * (NCH + 1)

PRE_LINKS = 44
MIX_LINKS = 99


def hybrid_kernel(nc, x, w_qkv0, w_out0, b_out0, w_qkvT, w_outT, b_out1, gn_w, gn_b, router_w, router_b,
                  expert_w, expert_b, consts, out, safe_bound=SAFE_BOUND, batches=B):
    x_v = x.rearrange("b y z c -> (b y z c)").rearrange("(b p n) -> b p n", b=B, p=P)
    out_v = out.rearrange("b y z c -> (b y z c)").rearrange("(b p n) -> b p n", b=B, p=P)

    ctx = ExitStack()
    with ctx:
        def sb(name, shape, dt=F32, stack=ctx):
            return stack.enter_context(nc.sbuf_tensor(name, shape, dt))

        def sem(name):
            return ctx.enter_context(nc.semaphore(name))

        def settle(engine):
            engine.sem_inc(s_settled, 1)

        X = sb("X", [P, T, C])
        XT = sb("XT", [P, N])
        QH = sb("QH", [P, N])
        QL = sb("QL", [P, N])
        KE = sb("KE", [P, 2 * N])
        V = sb("V", [P, T, C])
        KH, KL = KE[:, 0:N], KE[:, N:2 * N]
        E = KE[:, :].rearrange("p (r n) -> p r n", r=RING)
        ACC = XT[:, :].rearrange("p (g s n) -> p g s n", g=2, s=2)

        WQKV = sb("WQKV", [P, 3 * C])
        WOUT0 = sb("WOUT0", [P, C])
        WQKV1 = sb("WQKV1", [P, 3 * C])
        WOUT1 = sb("WOUT1", [P, C])
        WEXP = sb("WEXP", [P, EXPERTS, C])
        WR = sb("WR", [P, EXPERTS])
        RB = sb("RB", [P, EXPERTS])
        BO0 = sb("BO0", [P, C])
        BO1 = sb("BO1", [P, C])
        GNW = sb("GNW", [P, C])
        GNB = sb("GNB", [P, C])
        EB = sb("EB", [P, TPB, C])
        CONST = sb("CONST", [P, 6 * P])
        IDENT = CONST[:, 0:P]
        GAVG = CONST[:, P:2 * P]
        ONES = CONST[:, 2 * P:3 * P]
        NEG = CONST[:, 3 * P:4 * P]
        BLOCK = CONST[:, 4 * P:5 * P]
        RANK = CONST[:, 5 * P:5 * P + EXPERTS]

        ST = sb("ST", [P, T, 6])
        MV = sb("MV", [P, 2])
        SMALL = sb("SMALL", [P, 16])
        SS = sb("SS", [P, 2, NCH])
        MXS = sb("MXS", [P, 2, NCH])
        RT = sb("RT", [P, T])
        RU = sb("RU", [P, T])
        RA = sb("RA", [P, T])
        RY = sb("RY", [P, T])
        MEAN = sb("MEAN", [P, T])
        FLAG = sb("FLAG", [P, 1], I32)
        PVC = sb("PVC", [P, CH])
        REC = sb("REC", [P, CH])

        attn = ExitStack()
        KS = sb("KS", [P, H, N], F32R, attn)
        QS = sb("QS", [P, 2, H, CH], F32R, attn)
        RM = sb("RM", [P, H, CH], F32, attn)
        attn.close()
        mix = ExitStack()
        QE = sb("QE", [P, N], F32, mix)
        QT = sb("QT", [P, N], F32, mix)
        Y = sb("Y", [P, T, C], F32, mix)
        QM = sb("QM", [P, T * H], F32, mix)
        QSUM = sb("QSUM", [P, T * H], F32, mix)
        CTX = sb("CTX", [P, C], F32, mix)
        AT = sb("AT", [P, C], F32, mix)
        GA = sb("GA", [P, C], F32, mix)
        GB = sb("GB", [P, C], F32, mix)
        L = sb("L", [P, T, EXPERTS], F32, mix)
        PR = sb("PR", [P, T, EXPERTS], F32, mix)
        OH = sb("OH", [P, T, EXPERTS], F32, mix)
        TK = sb("TK", [P, T, EXPERTS], F32, mix)
        GT = sb("GT", [P, T, EXPERTS], F32, mix)
        G32 = sb("G32", [P, T, 32], F32, mix)
        GTT = sb("GTT", [P, NCH, P], F32, mix)
        R1 = sb("R1", [P, 4, T], F32, mix)
        mix.close()

        BK8 = ctx.enter_context(nc.psum_tensor("BK8", [P, 8, CH], F32))
        BK = [BK8[:, i, :] for i in range(8)]
        S = [BK8[:, 2 * i:2 * i + 2, :] for i in range(AHEAD)]
        PV, SM = BK[2 * AHEAD], BK[2 * AHEAD + 1]
        LATE = (STEPS - AHEAD) % AHEAD
        GS = S[LATE]

        s_settled = sem("s_settled")
        s_const = sem("s_const")
        s_x_in = [sem(f"s_x_in{i}") for i in range(4)]
        s_x_out = [sem(f"s_x_out{i}") for i in range(4)]
        s_eb0 = sem("s_eb0")
        s_eb = sem("s_eb")
        s_start = sem("s_start")
        s_xT = sem("s_xT")
        s_raw0 = sem("s_raw0")
        s_pre = sem("s_pre")
        s_cst = sem("s_cst")
        s_gm = sem("s_gm")
        s_gn = sem("s_gn")
        s_xn_act = sem("s_xn_act")
        s_xn_dve = sem("s_xn_dve")
        s_proj = sem("s_proj")
        s_sq = sem("s_sq")
        s_sqmax = sem("s_sqmax")
        s_kn = sem("s_kn")
        s_qh = sem("s_qh")
        s_kh = sem("s_kh")
        s_v = sem("s_v")
        s_flag = sem("s_flag")
        s_bias = sem("s_bias")
        s_k_in = sem("s_k_in")
        s_q_in = sem("s_q_in")
        s_scores = sem("s_scores")
        s_exp = sem("s_exp")
        s_pv = sem("s_pv")
        s_adds = sem("s_adds")
        s_sum = sem("s_sum")
        s_pvc = sem("s_pvc")
        s_rec = sem("s_rec")
        s_ot = sem("s_ot")
        s_gscore = sem("s_gscore")
        s_gmax = sem("s_gmax")
        s_gred = sem("s_gred")
        s_y0 = sem("s_y0")
        s_mix = sem("s_mix")
        s_z = sem("s_z")
        s_zT = sem("s_zT")
        s_zc_a = sem("s_zc_a")
        s_zc_d = sem("s_zc_d")
        s_k1 = sem("s_k1")
        s_k1c = sem("s_k1c")
        s_k1m = sem("s_k1m")
        s_k1x = sem("s_k1x")
        s_k1e = sem("s_k1e")
        s_v1 = sem("s_v1")
        s_v1c = sem("s_v1c")
        s_q1 = sem("s_q1")
        s_q1s = sem("s_q1s")
        s_q1e = sem("s_q1e")
        s_q1r = sem("s_q1r")
        s_q1n = sem("s_q1n")
        s_kT = sem("s_kT")
        s_kTc = sem("s_kTc")
        s_ctx = sem("s_ctx")
        s_at = sem("s_at")
        s_qT = sem("s_qT")
        s_qTc = sem("s_qTc")
        s_y1 = sem("s_y1")
        s_y1c = sem("s_y1c")
        s_bst = sem("s_bst")
        s_gst = sem("s_gst")
        s_gab = sem("s_gab")
        s_xb = sem("s_xb")
        s_route = sem("s_route")
        s_rt = sem("s_rt")
        s_rte = sem("s_rte")
        s_gate = sem("s_gate")
        s_gtT = sem("s_gtT")
        s_gtc = sem("s_gtc")
        s_ebm = sem("s_ebm")
        s_eba = sem("s_eba")
        s_ex = sem("s_ex")
        s_comb = sem("s_comb")

        COMB = (T // 2) * 2 * EXPERTS
        block = ctx.enter_context(nc.Block())

        @block.sync
        def _(sp):
            loads = [(WQKV[:, :], w_qkv0), (WOUT0[:, :], w_out0), (WQKV1[:, :], w_qkvT), (WOUT1[:, :], w_outT),
                     (WEXP[:, :, :], expert_w.rearrange("e d c -> d e c")), (WR[:, :], router_w),
                     (RB[:, :], router_b.partition_broadcast(P)), (BO0[:, :], b_out0.partition_broadcast(P)),
                     (BO1[:, :], b_out1.partition_broadcast(P)), (GNW[:, :], gn_w.partition_broadcast(P)),
                     (GNB[:, :], gn_b.partition_broadcast(P)), (CONST[:, :], consts)]
            for dst, src in loads:
                sp.dma_start(dst, src).then_inc(s_const, 16)
            sp.wait_ge(s_eb0, 1)
            for s in range(TPB):
                sp.dma_start(EB[32 * s:32 * s + EXPERTS, s, :], expert_b).then_inc(s_eb, 16)
            with sp.Fori(0, batches) as b:
                for i in range(4):
                    part = slice(i * T // 4 * C, (i + 1) * T // 4 * C)
                    sp.wait_ge(s_x_out[i], b * 16)
                    sp.dma_start(X[:, :, :].rearrange("p t c -> p (t c)")[:, part], x_v[b, :, part]).then_inc(s_x_in[i], 16)
                for r in range(4):
                    if r % 2 == 0:
                        sp.wait_ge(s_kh, b * 3 + 1 + r // 2)
                    for h in range(H):
                        src = KH if r < 2 else KL
                        sp.dma_start(KS[D * r:D * r + D, h, :].bitcast(F32), src[D * h:D * h + D, :]).then_inc(s_k_in, 16)
                sp.wait_ge(s_kh, b * 3 + 3)

                def load_q(c):
                    for r in range(4):
                        for h in range(H):
                            src = QH if r % 2 == 0 else QL
                            sp.dma_start(QS[D * r:D * r + D, c % 2, h, :].bitcast(F32),
                                         src[D * h:D * h + D, bass.ts(c, CH)]).then_inc(s_q_in, 16)

                load_q(0)
                sp.wait_ge(s_q_in, b * QLOADS + 256)
                load_q(1)
                with sp.Fori(2, NCH) as c:
                    sp.wait_ge(s_q_in, b * QLOADS + c * 256)
                    sp.wait_ge(s_scores, b * SCORED + (c * STEPS - STEPS))
                    load_q(c)
                sp.wait_ge(s_q_in, b * QLOADS + NCH * 256)
                sp.sem_inc(s_q_in, 256)
                for i in range(4):
                    part = slice(i * T // 4 * C, (i + 1) * T // 4 * C)
                    sp.wait_ge(s_comb, b * COMB + (i + 1) * COMB // 4)
                    sp.dma_start(out_v[b, :, part], X[:, :, :].rearrange("p t c -> p (t c)")[:, part]).then_inc(s_x_out[i], 16)
            for i in range(4):
                sp.wait_ge(s_x_out[i], batches * 16)

        @block.gpsimd
        def _(pool):
            nc.gpsimd.memset(EB[:, :, :], 0.0).then_inc(s_eb0, 1)
            pool.wait_ge(s_const, 12 * 16)
            pool.wait_ge(s_eb, TPB * 16)
            with pool.Fori(0, batches) as b:
                pool.wait_ge(s_xT, b * NCH + NCH)
                nc.gpsimd.tensor_tensor(X[:, :, :], X[:, :, :], BO0[:, :].unsqueeze(1).to_broadcast([P, T, C]),
                                        ALU.add).then_inc(s_bias, 1)
                pool.wait_ge(s_flag, b + 1)
                settle(pool)
                general = pool.value_load(FLAG[0:1, 0:1], min_val=0, max_val=1)
                with pool.If(general):
                    with pool.Fori(0, NCH + 1) as c:
                        pool.wait_ge(s_gmax, b * GEN + c * STEPS + STEPS)
                        settle(pool)
                        nc.gpsimd.partition_all_reduce(RM[:, :, :].rearrange("p h n -> p (h n)"),
                                                       RM[:, :, :].rearrange("p h n -> p (h n)"), P,
                                                       bass.bass_isa.ReduceOp.max).then_inc(s_gred, 1)
                with pool.Else():
                    pool.sem_inc(s_gred, NCH + 1)
                for c in range(NCH):
                    pool.wait_ge(s_q1r, b * NCH + c + 1)
                    q = QE[:, c * CH:(c + 1) * CH].rearrange("p (g d) -> p g d", d=D)
                    r = QSUM[:, c * TPB * H:(c + 1) * TPB * H].unsqueeze(2).to_broadcast([P, TPB * H, D])
                    nc.gpsimd.tensor_tensor(q, q, r, ALU.mult).then_inc(s_q1n, 1)
                pool.wait_ge(s_gab, b + 1)
                nc.gpsimd.tensor_tensor(X[:, :, :], X[:, :, :], GB[:, :].unsqueeze(1).to_broadcast([P, T, C]),
                                        ALU.add).then_inc(s_xb, 1)

        @block.scalar
        def _(act):
            with act.Fori(0, batches) as b:
                act.wait_ge(s_xT, b * NCH + 1)
                nc.scalar.activation(XT[:, 0:CH], BK[0], ACT.Copy).then_inc(s_raw0, 1)
                act.wait_ge(s_gn, b + 1)
                for c in range(1, NCH, 2):
                    nc.scalar.activation(XT[:, c * CH:(c + 1) * CH], BK[c], ACT.Identity,
                                         bias=SMALL[:, 4:5], scale=SMALL[:, 3:4]).then_inc(s_xn_act, 1)
                for i in range(2 * NCH):
                    c = i % NCH
                    act.wait_ge(s_proj, b * (3 * NCH) + i + 1)
                    raw = KL if i < NCH else QL
                    nc.scalar.activation(raw[:, c * CH:(c + 1) * CH], BK[c], ACT.Copy)
                    nc.scalar.activation(BK[c], BK[c], ACT.Square,
                                         accum_out=SS[:, i // NCH, c:c + 1]).then_inc(s_sq, 1)
                for c in range(NCH):
                    act.wait_ge(s_proj, b * (3 * NCH) + 2 * NCH + c + 1)
                    nc.scalar.activation(V[:, c * TPB:(c + 1) * TPB, :].rearrange("p t c -> p (t c)"), BK[c],
                                         ACT.Copy).then_inc(s_v, 1)
                act.wait_ge(s_kn, b + 1)
                nc.scalar.activation(QH[:, :].bitcast(F32R), QL[:, :], ACT.Copy,
                                     scale=SMALL[:, 7:8]).then_inc(s_qh, 1)
                act.wait_ge(s_k_in, b * 256 + 256)
                with act.Fori(0, NCH) as c:
                    for s in range(STEPS):
                        jt, p = s // 2, s % 2
                        if p == 0:
                            act.wait_ge(s_pv, b * (NCH * T) + c * T + jt + 1)
                            act.wait_ge(s_adds, b * (NCH * NG * ADDS) + c * (NG * ADDS)
                                        + ADDS * (jt // GROUP) + (2, 2, 4, 6)[jt % GROUP])
                        if s == 0 or s >= AHEAD:
                            act.wait_ge(s_scores, b * SCORED + c * STEPS + max(s + 1, AHEAD))
                        nc.scalar.activation(E[:, s % RING, :], S[s % AHEAD].rearrange("p a n -> p (a n)"), ACT.Exp,
                                             scale=SCALE0).then_inc(s_exp, 1)
                for c in range(0, NCH, 2):
                    act.wait_ge(s_zT, b * (2 * NCH) + c + 1)
                    nc.scalar.activation(XT[:, c * CH:(c + 1) * CH], BK[c], ACT.Copy).then_inc(s_zc_a, 1)
                for c in range(NCH):
                    act.wait_ge(s_k1, b * NCH + c + 1)
                    nc.scalar.activation(KH[:, c * CH:(c + 1) * CH], BK[c], ACT.Copy).then_inc(s_k1c, 1)
                act.wait_ge(s_k1x, b + 1)
                nc.scalar.activation(KH[:, :], KH[:, :], ACT.Exp, bias=SMALL[:, 8:9],
                                     accum_out=SMALL[:, 9:10]).then_inc(s_k1e, 1)
                for c in range(NCH):
                    act.wait_ge(s_v1, b * NCH + c + 1)
                    nc.scalar.activation(V[:, c * TPB:(c + 1) * TPB, :].rearrange("p t c -> p (t c)"), BK[c],
                                         ACT.Copy).then_inc(s_v1c, 1)
                for c in range(NCH):
                    act.wait_ge(s_q1s, b * NCH + c + 1)
                    nc.scalar.activation(QE[:, c * CH:(c + 1) * CH], QE[:, c * CH:(c + 1) * CH],
                                         ACT.Exp).then_inc(s_q1e, 1)
                for c in range(NCH):
                    act.wait_ge(s_kT, b * NCH + c + 1)
                    nc.scalar.activation(KL[:, c * CH:(c + 1) * CH], BK[c], ACT.Copy).then_inc(s_kTc, 1)
                for c in range(NCH):
                    act.wait_ge(s_qT, b * NCH + c + 1)
                    nc.scalar.activation(QT[:, c * CH:(c + 1) * CH], BK[c], ACT.Copy).then_inc(s_qTc, 1)
                for c in range(0, NCH, 2):
                    act.wait_ge(s_zT, b * (2 * NCH) + NCH + c + 1)
                    nc.scalar.activation(XT[:, c * CH:(c + 1) * CH], BK[c], ACT.Copy).then_inc(s_zc_a, 1)
                act.wait_ge(s_rt, b + 1)
                nc.scalar.activation(PR[:, :, :], PR[:, :, :], ACT.Exp).then_inc(s_rte, 1)

        @block.vector
        def _(dve):
            v = nc.vector

            def chain(done, before):
                n = [0]

                def link(instruction):
                    n[0] += 1
                    instruction.then_inc(done, 1)
                    dve.wait_ge(done, before + n[0])

                return link, n

            def rsqrt(link, y, a, n):
                t, u = RT[:, 0:n], RU[:, 0:n]
                link(v.tensor_scalar(t.bitcast(U32), a.bitcast(U32), 1, None, ALU.logical_shift_right))
                link(v.tensor_scalar(y.bitcast(I32), t.bitcast(I32), -1.0, float(MAGIC), ALU.mult, ALU.add))
                for _ in range(3):
                    link(v.tensor_tensor(u, y, y, ALU.mult))
                    link(v.scalar_tensor_tensor(u, u, -0.5, a, ALU.mult, ALU.mult))
                    link(v.scalar_tensor_tensor(y, u, 1.5, y, ALU.add, ALU.mult))

            def layernorm(mix_link, b, done):
                for t in range(T):
                    last = v.bn_stats(ST[:, t, :], X[:, t, :])
                mix_link(last)
                me, qe, mo, qo = (ST[:, :, i] for i in (1, 2, 4, 5))
                mix_link(v.tensor_tensor(MEAN[:, :], me, mo, ALU.add))
                mix_link(v.tensor_tensor(RA[:, :], me, mo, ALU.subtract))
                mix_link(v.tensor_tensor(RT[:, :], RA[:, :], RA[:, :], ALU.mult))
                mix_link(v.tensor_tensor(RU[:, :], qe, qo, ALU.add))
                mix_link(v.tensor_scalar(MEAN[:, :], MEAN[:, :], 0.5, None, ALU.mult))
                mix_link(v.tensor_scalar(RU[:, :], RU[:, :], 1.0 / C, 1e-5, ALU.mult, ALU.add))
                mix_link(v.scalar_tensor_tensor(RA[:, :], RT[:, :], 0.25, RU[:, :], ALU.mult, ALU.add))
                rsqrt(mix_link, RY[:, :], RA[:, :], T)
                for t in range(T):
                    last = v.tensor_scalar(QL[:, t * C:(t + 1) * C], X[:, t, :], MEAN[:, t:t + 1], RY[:, t:t + 1],
                                           ALU.subtract, ALU.mult)
                    if t % TPB == TPB - 1:
                        last.then_inc(s_z, 1)
                for c in range(1, NCH, 2):
                    dve.wait_ge(s_zT, b * (2 * NCH) + done * NCH + c + 1)
                    v.tensor_copy(XT[:, c * CH:(c + 1) * CH], BK[c]).then_inc(s_zc_d, 1)

            dve.sem_inc(s_adds, ADDS)
            dve.wait_ge(s_const, 12 * 16)
            with dve.Fori(0, batches) as b:
                pre_link, pre_n = chain(s_pre, b * PRE_LINKS)
                for c in (*range(1, NCH), 0):
                    if c:
                        dve.wait_ge(s_xT, b * NCH + c + 1)
                    else:
                        dve.wait_ge(s_raw0, b + 1)
                    last = v.bn_stats(ST[:, c, :], BK[c])
                pre_link(last)
                settle(dve)
                v.bn_aggr(MV[:, :], ST[:, 0:NCH, :].rearrange("p a s -> p (a s)")).then_inc(s_cst, 1)
                dve.wait_ge(s_gm, b * 3 + 1)
                pre_link(v.tensor_copy(SMALL[:, 0:1], BK[0][:, 0:1]))
                pre_link(v.tensor_tensor(SMALL[:, 1:2], MV[:, 0:1], SMALL[:, 0:1], ALU.subtract))
                v.scalar_tensor_tensor(SMALL[:, 2:3], SMALL[:, 1:2], SMALL[:, 1:2], MV[:, 1:2],
                                       ALU.mult, ALU.add).then_inc(s_cst, 1)
                dve.wait_ge(s_gm, b * 3 + 2)
                pre_link(v.tensor_scalar(RA[:, 0:1], BK[0][:, 1:2], 1e-5, None, ALU.add))
                rsqrt(pre_link, SMALL[:, 3:4], RA[:, 0:1], 1)
                v.scalar_tensor_tensor(SMALL[:, 4:5], SMALL[:, 0:1], -1.0, SMALL[:, 3:4],
                                       ALU.mult, ALU.mult).then_inc(s_gn, 1)
                for c in range(0, NCH, 2):
                    v.tensor_scalar(XT[:, c * CH:(c + 1) * CH], XT[:, 0:CH] if c == 0 else BK[c],
                                    SMALL[:, 0:1], SMALL[:, 3:4], ALU.subtract, ALU.mult).then_inc(s_xn_dve, 1)

                for m in range(2):
                    for c in range(NCH):
                        dve.wait_ge(s_sq, b * (2 * NCH) + m * NCH + c + 1)
                        v.reduce_max(MXS[:, m, c:c + 1], BK[c], X_AX).then_inc(s_sqmax, 1)
                    pre_link(v.reduce_sum(RA[:, 1:2], SS[:, m, :], X_AX))
                    pre_link(v.tensor_scalar(RA[:, 0:1], RA[:, 1:2], 1e-24, None, ALU.max))
                    rsqrt(pre_link, SMALL[:, 6 + m:7 + m], RA[:, 0:1], 1)
                    if m == 0:
                        v.tensor_scalar(KH.bitcast(F32R), KL, SMALL[:, 6:7], None, ALU.mult).then_inc(s_kh, 1)
                        dve.wait_ge(s_kh, b * 3 + 1)
                        v.scalar_tensor_tensor(KL.bitcast(F32R), KL, SMALL[:, 6:7], KH,
                                               ALU.mult, ALU.subtract).then_inc(s_kh, 1)
                    else:
                        dve.wait_ge(s_sqmax, b * (2 * NCH) + 2 * NCH)
                        pre_link(v.reduce_max(SMALL[:, 10:12], MXS[:, :, :], X_AX))
                        pre_link(v.tensor_tensor(SMALL[:, 12:14], SMALL[:, 6:8], SMALL[:, 6:8], ALU.mult))
                        pre_link(v.tensor_tensor(SMALL[:, 12:14], SMALL[:, 12:14], SMALL[:, 10:12], ALU.mult))
                        v.reduce_sum(SMALL[:, 14:15], SMALL[:, 12:14], X_AX).then_inc(s_kn, 1)
                        dve.wait_ge(s_qh, b + 1)
                        v.scalar_tensor_tensor(QL[:, :].bitcast(F32R), QL[:, :], SMALL[:, 7:8], QH[:, :],
                                               ALU.mult, ALU.subtract).then_inc(s_kh, 1)
                dve.wait_ge(s_gm, b * 3 + 3)
                v.tensor_scalar(FLAG[:, :], BK[0][:, 0:1], 2.0 * safe_bound / SCALE0, None,
                                ALU.is_gt).then_inc(s_flag, 1)
                dve.wait_ge(s_flag, b + 1)
                assert pre_n[0] == PRE_LINKS, pre_n

                def maxima(first):
                    for s in range(STEPS):
                        jt, p = s // 2, s % 2
                        dve.wait_ge(s_gscore, first + (s + 1))
                        rm = RM[:, 2 * p:2 * p + 2, :]
                        if jt == 0:
                            v.tensor_copy(rm, GS).then_inc(s_gmax, 1)
                        else:
                            dve.wait_ge(s_gmax, first + (s - 1))
                            v.tensor_tensor(rm, GS, rm, ALU.max).then_inc(s_gmax, 1)

                def attend(c, safe):
                    chunk = b * NCH + c
                    for g in range(NG):
                        if g == 1:
                            with dve.If(c):
                                normalise(chunk, c)
                        for k in range(1, GROUP):
                            for p in range(2):
                                done = 2 * (g * GROUP + k) + p
                                n = g * ADDS + 2 * (k - 1) + p
                                acc = ACC[:, g % 2, p, :]
                                if k == 1 and p == 0:
                                    dve.wait_ge(s_sum, chunk * NG + g + 1)
                                dve.wait_ge(s_exp, chunk * STEPS + done + 1)
                                if k == 1:
                                    one = E[:, (done - 2) % RING, :]
                                else:
                                    one = acc
                                    dve.wait_ge(s_adds, chunk * (NG * ADDS) + ADDS + n - 1)
                                v.tensor_tensor(acc, one, E[:, done % RING, :], ALU.add).then_inc(s_adds, 1)
                    if not safe:
                        maxima(b * GEN + c * STEPS + STEPS)
                    dve.wait_ge(s_pv, chunk * T + T + RING // 2)
                    v.tensor_copy(PVC[:, :], PV).then_inc(s_pvc, 1)

                def normalise(after, place):
                    dve.wait_ge(s_sum, after * NG + 2)
                    v.reciprocal(REC[:, :], SM).then_inc(s_rec, 1)
                    dve.wait_ge(s_pvc, after)
                    dve.wait_ge(s_rec, after)
                    v.tensor_tensor(QH[:, bass.ts(place, CH)], PVC[:, :], REC[:, :], ALU.mult).then_inc(s_ot, 1)
                    dve.wait_ge(s_ot, after)
                    settle(dve)

                settle(dve)
                general = dve.value_load(FLAG[0:1, 0:1], min_val=0, max_val=1)
                with dve.If(general):
                    maxima(b * GEN)
                    with dve.Fori(0, NCH) as c:
                        attend(c, False)
                    normalise(b * NCH + NCH, 0)
                with dve.Else():
                    dve.sem_inc(s_gmax, GEN)
                    with dve.Fori(0, NCH) as c:
                        attend(c, True)
                    normalise(b * NCH + NCH, 0)

                mix_link, mix_n = chain(s_mix, b * MIX_LINKS)
                dve.wait_ge(s_bias, b + 1)
                for c in range(NCH):
                    dve.wait_ge(s_y0, b * NCH + c + 1)
                    part = X[:, c * TPB:(c + 1) * TPB, :].rearrange("p t c -> p (t c)")
                    last = v.tensor_tensor(part, BK[c], part, ALU.add)
                mix_link(last)

                layernorm(mix_link, b, 0)
                for c in range(NCH):
                    dve.wait_ge(s_k1c, b * NCH + c + 1)
                    v.reduce_max(MXS[:, 0, c:c + 1], KH[:, c * CH:(c + 1) * CH], X_AX).then_inc(s_k1m, 1)
                dve.wait_ge(s_k1m, b * NCH + NCH)
                mix_link(v.reduce_max(SMALL[:, 10:11], MXS[:, 0, :], X_AX))
                v.tensor_scalar(SMALL[:, 8:9], SMALL[:, 10:11], -1.0, None, ALU.mult).then_inc(s_k1x, 1)
                for c in range(NCH):
                    g = slice(c * TPB * H, (c + 1) * TPB * H)
                    dve.wait_ge(s_q1, b * NCH + c + 1)
                    q = BK[c].rearrange("p (g d) -> p g d", d=D)
                    e = QE[:, c * CH:(c + 1) * CH].rearrange("p (g d) -> p g d", d=D)
                    mix_link(v.reduce_max(QM[:, g], q, X_AX))
                    v.tensor_tensor(e, q, QM[:, g].unsqueeze(2).to_broadcast([P, TPB * H, D]),
                                    ALU.subtract).then_inc(s_q1s, 1)
                for c in range(NCH):
                    g = slice(c * TPB * H, (c + 1) * TPB * H)
                    dve.wait_ge(s_q1e, b * NCH + c + 1)
                    mix_link(v.reduce_sum(QSUM[:, g], QE[:, c * CH:(c + 1) * CH].rearrange("p (g d) -> p g d", d=D), X_AX))
                    v.reciprocal(QSUM[:, g], QSUM[:, g]).then_inc(s_q1r, 1)
                dve.wait_ge(s_k1e, b + 1)
                mix_link(v.reciprocal(SMALL[:, 11:12], SMALL[:, 9:10]))
                dve.wait_ge(s_ctx, b * 2 + 1)
                v.scalar_tensor_tensor(CTX[:, :], BK[0][:, 0:C], SMALL[:, 11:12], BLOCK,
                                       ALU.mult, ALU.mult).then_inc(s_at, 1)
                dve.wait_ge(s_ctx, b * 2 + 2)
                v.tensor_copy(AT[:, :], BK[1][:, 0:C]).then_inc(s_at, 1)
                for c in range(NCH):
                    dve.wait_ge(s_y1, b * NCH + c + 1)
                    v.tensor_tensor(Y[:, c * TPB:(c + 1) * TPB, :], BK[c].rearrange("p (t c) -> p t c", c=C),
                                    BO1[:, :].unsqueeze(1).to_broadcast([P, TPB, C]), ALU.add).then_inc(s_y1c, 1)
                for c in range(NCH):
                    dve.wait_ge(s_y1c, b * NCH + c + 1)
                    last = v.bn_stats(ST[:, c, :], Y[:, c * TPB:(c + 1) * TPB, :].rearrange("p t c -> p (t c)"))
                mix_link(last)
                settle(dve)
                v.bn_aggr(MV[:, :], ST[:, 0:NCH, :].rearrange("p a s -> p (a s)")).then_inc(s_bst, 1)
                dve.wait_ge(s_gst, b * 2 + 1)
                mix_link(v.tensor_copy(SMALL[:, 0:1], BK[0][:, 0:1]))
                mix_link(v.tensor_tensor(SMALL[:, 1:2], MV[:, 0:1], SMALL[:, 0:1], ALU.add))
                v.scalar_tensor_tensor(SMALL[:, 2:3], SMALL[:, 1:2], SMALL[:, 1:2], MV[:, 1:2],
                                       ALU.mult, ALU.add).then_inc(s_bst, 1)
                dve.wait_ge(s_gst, b * 2 + 2)
                mix_link(v.tensor_scalar(RA[:, 0:1], BK[0][:, 1:2], -1.0, 1e-5, ALU.mult, ALU.add))
                rsqrt(mix_link, SMALL[:, 3:4], RA[:, 0:1], 1)
                mix_link(v.tensor_scalar(GA[:, :], GNW[:, :], SMALL[:, 3:4], None, ALU.mult))
                v.scalar_tensor_tensor(GB[:, :], GA[:, :], SMALL[:, 0:1], GNB[:, :], ALU.mult,
                                       ALU.add).then_inc(s_gab, 1)
                mix_link(v.tensor_tensor(Y[:, :, :], Y[:, :, :], GA[:, :].unsqueeze(1).to_broadcast([P, T, C]),
                                          ALU.mult))
                dve.wait_ge(s_xb, b + 1)
                mix_link(v.tensor_tensor(X[:, :, :], X[:, :, :], Y[:, :, :], ALU.add))

                layernorm(mix_link, b, 1)
                dve.wait_ge(s_route, b + 1)
                mix_link(v.tensor_tensor(L[:, :, :], BK[0][:, 0:T * EXPERTS].rearrange("p (t e) -> p t e", e=EXPERTS),
                                          RB[:, :].unsqueeze(1).to_broadcast([P, T, EXPERTS]), ALU.add))

                def over(x2):
                    return x2.unsqueeze(2).to_broadcast([P, T, EXPERTS])

                top, total, p1, p2 = (R1[:, i, :] for i in range(4))
                mix_link(v.reduce_max(top, L[:, :, :], X_AX))
                v.tensor_tensor(PR[:, :, :], L[:, :, :], over(top), ALU.subtract).then_inc(s_rt, 1)
                dve.wait_ge(s_rte, b + 1)
                mix_link(v.reduce_sum(total, PR[:, :, :], X_AX))
                mix_link(v.reciprocal(total, total))
                mix_link(v.tensor_tensor(PR[:, :, :], PR[:, :, :], over(total), ALU.mult))
                rank = RANK.unsqueeze(1).to_broadcast([P, T, EXPERTS])

                def pick(best, onehot):
                    mix_link(v.reduce_max(best, PR[:, :, :], X_AX))
                    mix_link(v.tensor_tensor(onehot, PR[:, :, :], over(best), ALU.is_equal))
                    mix_link(v.tensor_tensor(onehot, onehot, rank, ALU.mult))
                    mix_link(v.reduce_max(top, onehot, X_AX))
                    mix_link(v.tensor_tensor(onehot, rank, over(top), ALU.is_equal))

                pick(p1, OH[:, :, :])
                mix_link(v.scalar_tensor_tensor(PR[:, :, :], OH[:, :, :], -2.0, PR[:, :, :], ALU.mult, ALU.add))
                pick(p2, TK[:, :, :])
                mix_link(v.tensor_tensor(total, p1, p2, ALU.add))
                mix_link(v.reciprocal(total, total))
                mix_link(v.tensor_tensor(p1, p1, total, ALU.mult))
                mix_link(v.tensor_tensor(p2, p2, total, ALU.mult))
                mix_link(v.tensor_tensor(OH[:, :, :], OH[:, :, :], over(p1), ALU.mult))
                mix_link(v.tensor_tensor(TK[:, :, :], TK[:, :, :], over(p2), ALU.mult))
                mix_link(v.tensor_tensor(GT[:, :, :], OH[:, :, :], TK[:, :, :], ALU.add))
                mix_link(v.memset(G32[:, :, :], 0.0))
                v.tensor_copy(G32[:, :, 0:EXPERTS], GT[:, :, :]).then_inc(s_gate, 1)
                for i in range(2):
                    dve.wait_ge(s_gtT, b * 2 + i + 1)
                    v.tensor_copy(GTT[:, 4 * i:4 * i + 4, :].rearrange("p a n -> p (a n)"), BK[i]).then_inc(s_gtc, 1)
                for c in range(NCH):
                    dve.wait_ge(s_ebm, b * NCH + c + 1)
                    part = X[:, c * TPB:(c + 1) * TPB, :].rearrange("p t c -> p (t c)")
                    v.tensor_tensor(part, BK[c], part, ALU.add).then_inc(s_eba, 1)
                dve.wait_ge(s_eba, b * NCH + NCH)
                for i in range(T // 2):
                    dve.wait_ge(s_ex, b * (T // 2) + i + 1)
                    for e in range(EXPERTS):
                        for u in range(2):
                            t, n = 2 * i + u, (i * EXPERTS + e) * 2 + u
                            y = BK8[:, 4 * (i % 2) + 2 * u + e // 4, (e % 4) * C:(e % 4 + 1) * C]
                            if e:
                                dve.wait_ge(s_comb, b * COMB + n - 1)
                            v.scalar_tensor_tensor(X[:, t, :], y, GT[:, t, e:e + 1], X[:, t, :],
                                                   ALU.mult, ALU.add).then_inc(s_comb, 1)
                assert mix_n[0] == MIX_LINKS, mix_n

        @block.tensor
        def _(pe):
            def mm(o, lhsT, rhs, start=True, stop=True, shared=False):
                return nc.tensor.matmul(o, lhsT, rhs, start=start, stop=stop, skip_group_check=shared)

            def transposes(dst, src, c):
                for t in range(c * TPB, (c + 1) * TPB):
                    last = nc.tensor.transpose(dst[:, (t % TPB) * P:(t % TPB + 1) * P], src(t), IDENT)
                return last

            pe.sem_inc(s_pv, RING // 2)
            pe.sem_inc(s_sum, 2)
            pe.wait_ge(s_const, 12 * 16)
            pe.wait_ge(s_eb, TPB * 16)
            with pe.Fori(0, batches) as b:
                pe.wait_ge(s_comb, b * COMB)
                for c in range(NCH):
                    if c % 2 == 0:
                        pe.wait_ge(s_x_in[c // 2], b * 16 + 16)
                    transposes(BK[c], lambda t: X[:, t, :], c).then_inc(s_xT, 1)
                pe.wait_ge(s_raw0, b + 1)
                pe.wait_ge(s_cst, b * 2 + 1)
                mm(BK[0][:, 0:1], GAVG, MV[:, 0:1]).then_inc(s_gm, 1)
                pe.wait_ge(s_cst, b * 2 + 2)
                mm(BK[0][:, 1:2], GAVG, SMALL[:, 2:3]).then_inc(s_gm, 1)
                for i, m in enumerate((1, 0)):
                    for c in range(NCH):
                        if i == 0:
                            if c % 2:
                                pe.wait_ge(s_xn_act, b * 4 + (c + 1) // 2)
                            else:
                                pe.wait_ge(s_xn_dve, b * 4 + c // 2 + 1)
                        else:
                            pe.wait_ge(s_sqmax, b * (2 * NCH) + c + 1)
                        mm(BK[c], WQKV[:, m * C:(m + 1) * C], XT[:, c * CH:(c + 1) * CH]).then_inc(s_proj, 1)
                for c in range(NCH):
                    pe.wait_ge(s_sqmax, b * (2 * NCH) + NCH + c + 1)
                    for t in range(c * TPB, (c + 1) * TPB):
                        last = mm(BK[c][:, (t % TPB) * C:(t % TPB + 1) * C], XT[:, t * P:(t + 1) * P], WQKV[:, 2 * C:3 * C])
                    last.then_inc(s_proj, 1)
                pe.wait_ge(s_kn, b + 1)
                pe.wait_ge(s_v, b * NCH + NCH)
                mm(BK[0][:, 0:1], ONES, SMALL[:, 14:15]).then_inc(s_gm, 1)
                pe.wait_ge(s_flag, b + 1)

                def scores(s, par, safe):
                    jt, p = s // 2, s % 2
                    for i in range(2):
                        h = 2 * p + i
                        last = mm(S[s % AHEAD][:, i, :], KS[:, h, jt * P:(jt + 1) * P],
                                  QS[:, par, h, :], stop=safe)
                        if not safe:
                            last = mm(S[s % AHEAD][:, i, :], NEG, RM[:, h, :], start=False)
                    return last

                def maxima(par, first, reds):
                    for s in range(STEPS):
                        jt, p = s // 2, s % 2
                        pe.wait_ge(s_gmax, first + s)
                        for i in range(2):
                            last = mm(GS[:, i, :], KS[:, 2 * p + i, jt * P:(jt + 1) * P], QS[:, par, 2 * p + i, :])
                        last.then_inc(s_gscore, 1)
                    pe.wait_ge(s_gred, reds)

                def values(jt):
                    for h in range(H):
                        e = E[:, (2 * jt + h // 2) % RING, (h % 2) * CH:(h % 2 + 1) * CH]
                        last = mm(PV[D * h:D * h + D, :], V[:, jt, D * h:D * h + D], e, start=(jt == 0), stop=(jt == T - 1))
                    last.then_inc(s_pv, 1)

                def sums(g, adds):
                    pe.wait_ge(s_adds, adds)
                    for h in range(H):
                        a = ACC[:, g % 2, h // 2, (h % 2) * CH:(h % 2 + 1) * CH]
                        last = mm(SM[D * h:D * h + D, :], ONES[:, 0:D], a, start=(g == 0), stop=(g == NG - 1))
                    last.then_inc(s_sum, 1)

                early = [(STEPS - AHEAD + i) % AHEAD for i in range(AHEAD)]

                def attend(c, safe):
                    chunk = b * NCH + c
                    for s in range(STEPS):
                        jt = s // 2
                        pe.wait_ge(s_exp, chunk * STEPS + s + 1)
                        if s == STEPS - AHEAD:
                            pe.wait_ge(s_q_in, b * QLOADS + (c + 2) * 256)
                            if not safe:
                                maxima((c + 1) % 2, b * GEN + c * STEPS + STEPS, b * (NCH + 1) + c + 2)
                        if s < STEPS - AHEAD:
                            last = scores(s + AHEAD, c % 2, safe)
                        else:
                            last = scores(early[s + AHEAD - STEPS], (c + 1) % 2, safe)
                        last.then_inc(s_scores, 1)
                        if s % 2:
                            if jt == 0:
                                pe.wait_ge(s_pvc, chunk)
                            values(jt)
                            if s == 3:
                                with pe.If(c):
                                    sums(NG - 1, chunk * (NG * ADDS) + ADDS)
                            if s >= 2 * GROUP + 5 and (s - 5) % (2 * GROUP) == 0:
                                g = (s - 5) // (2 * GROUP) - 1
                                if g == 0:
                                    pe.wait_ge(s_rec, chunk)
                                sums(g, chunk * (NG * ADDS) + (g + 2) * ADDS)

                pe.wait_ge(s_k_in, b * 256 + 256)
                pe.wait_ge(s_q_in, b * QLOADS + 256)
                settle(pe)
                general = pe.value_load(FLAG[0:1, 0:1], min_val=0, max_val=1)
                with pe.If(general):
                    maxima(0, b * GEN, b * (NCH + 1) + 1)
                    for s in early:
                        scores(s, 0, False).then_inc(s_scores, 1)
                    with pe.Fori(0, NCH) as c:
                        attend(c, False)
                    sums(NG - 1, (b * NCH + NCH) * (NG * ADDS) + ADDS)
                with pe.Else():
                    pe.sem_inc(s_gscore, GEN)
                    for s in early:
                        scores(s, 0, True).then_inc(s_scores, 1)
                    with pe.Fori(0, NCH) as c:
                        attend(c, True)
                    sums(NG - 1, (b * NCH + NCH) * (NG * ADDS) + ADDS)

                def tiles(lhsT, rhs, signal, before=None, onto=None):
                    for c in range(NCH):
                        if before:
                            before(c)
                        for t in range(c * TPB, (c + 1) * TPB):
                            last = mm(BK[c][:, (t % TPB) * C:(t % TPB + 1) * C], lhsT(t), rhs(t))
                        last.then_inc(signal, 1)

                pe.wait_ge(s_ot, b * NCH + NCH)
                tiles(lambda t: QH[:, (t + TPB) % T * P:((t + TPB) % T + 1) * P], lambda t: WOUT0[:, :], s_y0)

                def transposed(done):
                    for c in range(NCH):
                        pe.wait_ge(s_z, b * (2 * NCH) + done * NCH + c + 1)
                        transposes(BK[c], lambda t: QL[:, t * C:(t + 1) * C], c).then_inc(s_zT, 1)

                def xt(done):
                    def wait(c):
                        if c % 2:
                            pe.wait_ge(s_zc_d, b * NCH + done * 4 + (c + 1) // 2)
                        else:
                            pe.wait_ge(s_zc_a, b * NCH + done * 4 + c // 2 + 1)
                    return wait

                transposed(0)
                for c in range(NCH):
                    xt(0)(c)
                    mm(BK[c], WQKV1[:, C:2 * C], XT[:, c * CH:(c + 1) * CH]).then_inc(s_k1, 1)

                tiles(lambda t: XT[:, t * P:(t + 1) * P], lambda t: WQKV1[:, 2 * C:3 * C], s_v1,
                      lambda c: pe.wait_ge(s_k1c, b * NCH + c + 1))
                tiles(lambda t: XT[:, t * P:(t + 1) * P], lambda t: WQKV1[:, 0:C], s_q1,
                      lambda c: pe.wait_ge(s_v1c, b * NCH + c + 1))
                pe.wait_ge(s_k1e, b + 1)
                for c in range(NCH):
                    pe.wait_ge(s_q1s, b * NCH + c + 1)
                    transposes(BK[c], lambda t: KH[:, t * P:(t + 1) * P], c).then_inc(s_kT, 1)
                for t in range(T):
                    if t % TPB == 0:
                        pe.wait_ge(s_kTc, b * NCH + t // TPB + 1)
                    last = mm(BK[0][:, 0:C], KL[:, t * P:(t + 1) * P], V[:, t, :], start=(t == 0), stop=(t == T - 1))
                last.then_inc(s_ctx, 1)
                pe.wait_ge(s_at, b * 2 + 1)
                mm(BK[1][:, 0:C], CTX[:, :], WOUT1[:, :]).then_inc(s_ctx, 1)
                pe.wait_ge(s_at, b * 2 + 2)
                for c in range(NCH):
                    pe.wait_ge(s_q1n, b * NCH + c + 1)
                    transposes(BK[c], lambda t: QE[:, t * P:(t + 1) * P], c).then_inc(s_qT, 1)
                tiles(lambda t: QT[:, t * P:(t + 1) * P], lambda t: AT[:, :], s_y1,
                      lambda c: pe.wait_ge(s_qTc, b * NCH + c + 1))
                pe.wait_ge(s_bst, b * 2 + 1)
                mm(BK[0][:, 0:1], NEG, MV[:, 0:1]).then_inc(s_gst, 1)
                pe.wait_ge(s_bst, b * 2 + 2)
                mm(BK[0][:, 1:2], NEG, SMALL[:, 2:3]).then_inc(s_gst, 1)

                transposed(1)
                for c in range(NCH - 2, NCH):
                    xt(1)(c)
                for t in range(T):
                    last = mm(BK[0][:, t * EXPERTS:(t + 1) * EXPERTS], XT[:, t * P:(t + 1) * P], WR[:, :])
                last.then_inc(s_route, 1)
                pe.wait_ge(s_gate, b + 1)
                for i in range(2):
                    for k in range(4):
                        a = 4 * i + k
                        last = nc.tensor.transpose(BK[i][:, k * P:(k + 1) * P],
                                                   G32[:, TPB * a:TPB * (a + 1), :].rearrange("p t e -> p (t e)"), IDENT)
                    last.then_inc(s_gtT, 1)
                pe.wait_ge(s_gtc, b * 2 + 2)
                tiles(lambda t: GTT[:, t // TPB, :], lambda t: EB[:, t % TPB, :], s_ebm)
                for i in range(T // 2):
                    if i < 2:
                        pe.wait_ge(s_eba, b * NCH + 4 * i + 4)
                    else:
                        pe.wait_ge(s_comb, b * COMB + (i - 1) * 2 * EXPERTS)
                    for u in range(2):
                        t = 2 * i + u
                        for half in range(2):
                            last = mm(BK[4 * (i % 2) + 2 * u + half], XT[:, t * P:(t + 1) * P],
                                      WEXP[:, half * 4:half * 4 + 4, :].rearrange("p e c -> p (e c)"))
                    last.then_inc(s_ex, 1)


_INS = ["x", "L0_conv_w_qkv", "L0_conv_w_out", "L0_conv_b_out", "L1_attn_W_qkv", "L1_attn_W_out", "L1_attn_b_out",
        "L1_attn_gn_w", "L1_attn_gn_b", "L1_ffn_router_w", "L1_ffn_router_b", "L1_ffn_expert_w", "L1_ffn_expert_b"]


def constants():
    i = np.arange(P)
    per = C // G
    rank = np.zeros((P, P))
    rank[:, 0:EXPERTS] = EXPERTS - np.arange(EXPERTS)
    return np.concatenate([
        np.eye(P), (i[:, None] // per == i[None, :] // per) / per, np.ones((P, P)), np.full((P, P), -1.0 / P),
        (i[:, None] // D == i[None, :] // D) * SCALE1, rank], axis=1).astype(np.float32)


def kernel(**inputs):
    import concourse.bacc as bacc
    from concourse.bass_utils import run_bass_kernel_spmd

    nc = bacc.Bacc("TRN2", target_bir_lowering=False, num_devices=1, dynamic_dma_scratch_size=1024)
    given = {n: np.asarray(inputs[n]) for n in _INS}
    for n in ("L1_attn_W_qkv", "L1_attn_W_out"):
        given[n] = given[n].T
    given["consts"] = constants()
    arrays, args = {}, []
    for n, a in given.items():
        arrays[f"in_{n}"] = np.ascontiguousarray(a)
        args.append(nc.dram_tensor(f"in_{n}", a.shape, mybir.dt.from_np(a.dtype), kind="ExternalInput").ap())
    args.append(nc.dram_tensor("out_0", (B, 64, 64, C), F32, kind="ExternalOutput").ap())
    hybrid_kernel(nc, *args)
    r = run_bass_kernel_spmd(nc, [arrays], core_ids=[0])
    return np.asarray(r.results[0]["out_0"])
```

```python
import numpy as np
import concourse.bass as bass
from concourse import mybir
from contextlib import ExitStack

F32 = mybir.dt.float32
F32R = mybir.dt.float32r
U32 = mybir.dt.uint32
I32 = mybir.dt.int32
ALU = mybir.AluOpType
ACT = mybir.ActivationFunctionType
X_AX = mybir.AxisListType.X

P = 128
B = 4
N = 64 * 64
C = 128
T = N // P
H = 4
D = C // H
CH = 512
NCH = N // CH
TPB = CH // P
G = 32
EXPERTS = 8
SCALE0 = 10.0
SCALE1 = D ** -0.5
SAFE_BOUND = 40.0
MAGIC = 0x5F3759DF

STEPS = 2 * T
AHEAD = 3
SCORED = STEPS * NCH + AHEAD
RING = 8
GROUPS = (5, 5, 5, 5, 6, 6)
NG = len(GROUPS)
FIRST = [sum(GROUPS[:g]) for g in range(NG)]
END = [sum(GROUPS[:g + 1]) for g in range(NG)]
ADDS = 2 * (T - NG)
ADDS0 = 2 * (GROUPS[-1] - 1)
LAG = 3
NORMALISED = 6
QLOADS = (NCH + 1) * 16 * 4 * H
GEN = STEPS * (NCH + 1)



def adds_until(j):
    if j < 0:
        return adds_until(T + j) - ADDS
    g = max(g for g in range(NG) if FIRST[g] <= j)
    return 2 * (FIRST[g] - g + max(j - FIRST[g], 1))


HALF = T // 2
HCH = NCH // 2
NDVE = EXPERTS // 2
EBUF = 3

PRE_LINKS = 45
MIX_LINKS = 136


def hybrid_kernel(nc, x, w_qkv0, w_out0, b_out0, w_qkvT, w_outT, b_out1, gn_w, gn_b, router_w, router_b,
                  expert_w, expert_b, consts, out, safe_bound=SAFE_BOUND, batches=B):
    x_v = x.rearrange("b y z c -> (b y z c)").rearrange("(b p n) -> b p n", b=B, p=P)
    out_v = out.rearrange("b y z c -> (b y z c)").rearrange("(b p n) -> b p n", b=B, p=P)

    ctx = ExitStack()
    with ctx:
        def sb(name, shape, dt=F32, stack=ctx):
            return stack.enter_context(nc.sbuf_tensor(name, shape, dt))

        def sem(name):
            return ctx.enter_context(nc.semaphore(name))

        def settle(engine):
            engine.sem_inc(s_settled, 1)

        X = sb("X", [P, T, C])
        XT = sb("XT", [P, N])
        QH = sb("QH", [P, N])
        QL = sb("QL", [P, N])
        KE = sb("KE", [P, 2 * N])
        V = sb("V", [P, T, C])
        KH, KL = KE[:, 0:N], KE[:, N:2 * N]
        E = KE[:, :].rearrange("p (r n) -> p r n", r=RING)
        ACC = XT[:, :].rearrange("p (g s n) -> p g s n", g=2, s=2)

        WQKV = sb("WQKV", [P, 3 * C])
        WOUT0 = sb("WOUT0", [P, C])
        WQKV1 = sb("WQKV1", [P, 3 * C])
        WOUT1 = sb("WOUT1", [P, C])
        WEXP = sb("WEXP", [P, EXPERTS, C])
        WR = sb("WR", [P, EXPERTS])
        RB = sb("RB", [P, EXPERTS])
        BO0 = sb("BO0", [P, C])
        BO1 = sb("BO1", [P, C])
        GNW = sb("GNW", [P, C])
        GNB = sb("GNB", [P, C])
        EB = sb("EB", [P, TPB, C])
        CONST = sb("CONST", [P, 6 * P])
        IDENT = CONST[:, 0:P]
        GAVG = CONST[:, P:2 * P]
        ONES = CONST[:, 2 * P:3 * P]
        NEG = CONST[:, 3 * P:4 * P]
        BLOCK = CONST[:, 4 * P:5 * P]
        RANK = CONST[:, 5 * P:5 * P + EXPERTS]

        ST = sb("ST", [P, T, 6])
        MV = sb("MV", [P, 2])
        SMALL = sb("SMALL", [P, 16])
        SS = sb("SS", [P, 2, NCH])
        MXS = sb("MXS", [P, 2, NCH])
        RT = sb("RT", [P, T])
        RU = sb("RU", [P, T])
        RA = sb("RA", [P, T])
        RY = sb("RY", [P, T])
        MEAN = sb("MEAN", [P, T])
        FLAG = sb("FLAG", [P, 1], I32)
        PVC = sb("PVC", [P, CH])
        REC = sb("REC", [P, CH])

        attn = ExitStack()
        KS = sb("KS", [P, H, N], F32R, attn)
        QS = sb("QS", [P, 2, H, CH], F32R, attn)
        RM = sb("RM", [P, H, CH], F32, attn)
        attn.close()
        mix = ExitStack()
        QE = sb("QE", [P, N], F32, mix)
        QT = sb("QT", [P, N], F32, mix)
        XN = sb("XN", [P, T, C], F32, mix)
        ZX = sb("ZX", [P, 2, 2, NDVE * C], F32, mix)
        Z2 = sb("Z2", [P, 2, 2 * C], F32, mix)
        NM = sb("NM", [P, T], F32, mix)
        QM = sb("QM", [P, T * H], F32, mix)
        QSUM = sb("QSUM", [P, T * H], F32, mix)
        CTX = sb("CTX", [P, C], F32, mix)
        AT = sb("AT", [P, C], F32, mix)
        AT2 = sb("AT2", [P, C], F32, mix)
        GA = sb("GA", [P, C], F32, mix)
        GB = sb("GB", [P, C], F32, mix)
        L = sb("L", [P, T, EXPERTS], F32, mix)
        PR = sb("PR", [P, T, EXPERTS], F32, mix)
        OH = sb("OH", [P, T, EXPERTS], F32, mix)
        TK = sb("TK", [P, T, EXPERTS], F32, mix)
        GT = sb("GT", [P, T, EXPERTS], F32, mix)
        G32 = sb("G32", [P, T, 32], F32, mix)
        GTT = sb("GTT", [P, NCH, P], F32, mix)
        R1 = sb("R1", [P, 4, T], F32, mix)
        mix.close()

        BK8 = ctx.enter_context(nc.psum_tensor("BK8", [P, 8, CH], F32))
        BK = [BK8[:, i, :] for i in range(8)]
        S = [BK8[:, 2 * i:2 * i + 2, :] for i in range(AHEAD)]
        PV, SM = BK[2 * AHEAD], BK[2 * AHEAD + 1]
        LATE = (STEPS - AHEAD) % AHEAD
        GS = S[LATE]

        s_settled = sem("s_settled")
        s_const = sem("s_const")
        s_x_in = [sem(f"s_x_in{i}") for i in range(4)]
        s_x_out = [sem(f"s_x_out{i}") for i in range(4)]
        s_eb0 = sem("s_eb0")
        s_eb = sem("s_eb")
        s_start = sem("s_start")
        s_xT = sem("s_xT")
        s_raw0 = sem("s_raw0")
        s_pre = sem("s_pre")
        s_cst = sem("s_cst")
        s_gm = sem("s_gm")
        s_gn = sem("s_gn")
        s_xn_act = sem("s_xn_act")
        s_xn_dve = sem("s_xn_dve")
        s_proj = sem("s_proj")
        s_sq = sem("s_sq")
        s_sqmax = sem("s_sqmax")
        s_kn = sem("s_kn")
        s_qh = sem("s_qh")
        s_kh = sem("s_kh")
        s_v = sem("s_v")
        s_flag = sem("s_flag")
        s_bias = sem("s_bias")
        s_k_in = sem("s_k_in")
        s_q_in = sem("s_q_in")
        s_scores = sem("s_scores")
        s_exp = sem("s_exp")
        s_pv = sem("s_pv")
        s_adds = sem("s_adds")
        s_sum = sem("s_sum")
        s_pvc = sem("s_pvc")
        s_rec = sem("s_rec")
        s_ot = sem("s_ot")
        s_gscore = sem("s_gscore")
        s_gmax = sem("s_gmax")
        s_gred = sem("s_gred")
        s_y0 = sem("s_y0")
        s_mix = sem("s_mix")
        s_x0 = sem("s_x0")
        s_x1 = sem("s_x1")
        s_ln = sem("s_ln")
        s_z_d = sem("s_z_d")
        s_z_a = sem("s_z_a")
        s_zT = sem("s_zT")
        s_zc = sem("s_zc")
        s_k1 = sem("s_k1")
        s_k1c = sem("s_k1c")
        s_k1m = sem("s_k1m")
        s_k1x = sem("s_k1x")
        s_k1e = sem("s_k1e")
        s_v1 = sem("s_v1")
        s_v1c = sem("s_v1c")
        s_q1 = sem("s_q1")
        s_q1s = sem("s_q1s")
        s_q1e = sem("s_q1e")
        s_q1r = sem("s_q1r")
        s_q1n = sem("s_q1n")
        s_kT = sem("s_kT")
        s_kTc = sem("s_kTc")
        s_ctx = sem("s_ctx")
        s_at = sem("s_at")
        s_qT = sem("s_qT")
        s_qTc = sem("s_qTc")
        s_y1 = sem("s_y1")
        s_y2 = sem("s_y2")
        s_bst = sem("s_bst")
        s_gst = sem("s_gst")
        s_route = sem("s_route")
        s_rt = sem("s_rt")
        s_rte = sem("s_rte")
        s_gate = sem("s_gate")
        s_gtT = sem("s_gtT")
        s_gtc = sem("s_gtc")
        s_ebm = sem("s_ebm")
        s_eba = sem("s_eba")
        s_ex = sem("s_ex")
        s_comb = sem("s_comb")
        s_zx = sem("s_zx")
        s_zs = sem("s_zs")

        COMB = T * NDVE
        PAIRS = T // 2 * 3

        def expert_bank(t, part):
            return BK[1 + 2 * (t % EBUF) + part]

        q_order = (*range(1, NCH), 0)

        block = ctx.enter_context(nc.Block())

        @block.sync
        def _(sp):
            loads = [(WQKV[:, :], w_qkv0), (WOUT0[:, :], w_out0), (WQKV1[:, :], w_qkvT), (WOUT1[:, :], w_outT),
                     (WEXP[:, :, :], expert_w.rearrange("e d c -> d e c")), (WR[:, :], router_w),
                     (RB[:, :], router_b.partition_broadcast(P)), (BO0[:, :], b_out0.partition_broadcast(P)),
                     (BO1[:, :], b_out1.partition_broadcast(P)), (GNW[:, :], gn_w.partition_broadcast(P)),
                     (GNB[:, :], gn_b.partition_broadcast(P)), (CONST[:, :], consts)]
            for dst, src in loads:
                sp.dma_start(dst, src).then_inc(s_const, 16)
            sp.wait_ge(s_eb0, 1)
            for s in range(TPB):
                sp.dma_start(EB[32 * s:32 * s + EXPERTS, s, :], expert_b).then_inc(s_eb, 16)

            def load_x(b):
                for i in range(4):
                    part = slice(i * T // 4 * C, (i + 1) * T // 4 * C)
                    sp.dma_start(XN[:, :, :].rearrange("p t c -> p (t c)")[:, part], x_v[b, :, part]).then_inc(s_x_in[i], 16)

            def stack(b):
                sp.wait_ge(s_bias, b * 4 + 4)
                settle(sp)
                for r in range(4):
                    if r % 2 == 0:
                        sp.wait_ge(s_kh, b * 4 + 1 + r // 2)
                    for h in range(H):
                        src = KH if r < 2 else KL
                        sp.dma_start(KS[D * r:D * r + D, h, :].bitcast(F32), src[D * h:D * h + D, :]).then_inc(s_k_in, 16)
                sp.wait_ge(s_kh, b * 4 + 3)

                def load_q(c):
                    for r in range(4):
                        for h in range(H):
                            src = QH if r % 2 == 0 else QL
                            sp.dma_start(QS[D * r:D * r + D, c % 2, h, :].bitcast(F32),
                                         src[D * h:D * h + D, bass.ts(c, CH)]).then_inc(s_q_in, 16)

                load_q(0)
                sp.wait_ge(s_q_in, b * QLOADS + 256)
                sp.wait_ge(s_kh, b * 4 + 4)
                load_q(1)
                with sp.Fori(2, NCH) as c:
                    sp.wait_ge(s_q_in, b * QLOADS + c * 256)
                    sp.wait_ge(s_scores, b * SCORED + (c * STEPS - STEPS))
                    load_q(c)
                sp.wait_ge(s_q_in, b * QLOADS + NCH * 256)
                sp.sem_inc(s_q_in, 256)

            def store(b):
                for i in range(4):
                    part = slice(i * T // 4 * C, (i + 1) * T // 4 * C)
                    sp.wait_ge(s_zs, b * PAIRS + (i + 1) * PAIRS // 4)
                    sp.dma_start(out_v[b, :, part], X[:, :, :].rearrange("p t c -> p (t c)")[:, part]).then_inc(s_x_out[i], 16)

            load_x(0)
            with sp.Fori(0, batches - 1) as b:
                stack(b)
                sp.wait_ge(s_scores, b * SCORED + SCORED)
                load_x(b + 1)
                store(b)
            stack(batches - 1)
            store(batches - 1)
            for i in range(4):
                sp.wait_ge(s_x_out[i], batches * 16)

        @block.gpsimd
        def _(pool):
            nc.gpsimd.memset(EB[:, :, :], 0.0).then_inc(s_eb0, 1)
            pool.wait_ge(s_const, 12 * 16)
            pool.wait_ge(s_eb, TPB * 16)
            with pool.Fori(0, batches) as b:
                with pool.If(b):
                    for i in range(4):
                        pool.wait_ge(s_x_out[i], b * 16)
                    settle(pool)
                for i in range(4):
                    part = slice(i * T // 4, (i + 1) * T // 4)
                    pool.wait_ge(s_x_in[i], b * 16 + 16)
                    nc.gpsimd.tensor_tensor(X[:, part, :], XN[:, part, :],
                                            BO0[:, :].unsqueeze(1).to_broadcast([P, T // 4, C]), ALU.add).then_inc(s_bias, 1)
                pool.wait_ge(s_flag, b + 1)
                settle(pool)
                general = pool.value_load(FLAG[0:1, 0:1], min_val=0, max_val=1)
                with pool.If(general):
                    with pool.Fori(0, NCH + 1) as c:
                        pool.wait_ge(s_gmax, b * GEN + c * STEPS + (STEPS + 1))
                        settle(pool)
                        nc.gpsimd.partition_all_reduce(RM[:, :, :].rearrange("p h n -> p (h n)"),
                                                       RM[:, :, :].rearrange("p h n -> p (h n)"), P,
                                                       bass.bass_isa.ReduceOp.max).then_inc(s_gred, 1)
                with pool.Else():
                    pool.sem_inc(s_gred, NCH + 1)
                for i, c in enumerate(q_order):
                    pool.wait_ge(s_q1r, b * NCH + i + 1)
                    q = QE[:, c * CH:(c + 1) * CH].rearrange("p (g d) -> p g d", d=D)
                    r = QSUM[:, c * TPB * H:(c + 1) * TPB * H].unsqueeze(2).to_broadcast([P, TPB * H, D])
                    nc.gpsimd.tensor_tensor(q, q, r, ALU.mult).then_inc(s_q1n, 1)
                for i in range(T // 2):
                    pool.wait_ge(s_zx, b * T + 2 * i + 2)
                    z = ZX[:, i % 2, :, :]
                    n = b * PAIRS + 3 * i
                    if i:
                        pool.wait_ge(s_zs, n)
                    nc.gpsimd.tensor_tensor(Z2[:, :, :], z[:, :, 0:2 * C], z[:, :, 2 * C:4 * C], ALU.add).then_inc(s_zs, 1)
                    pool.wait_ge(s_zs, n + 1)
                    nc.gpsimd.tensor_tensor(Z2[:, :, 0:C], Z2[:, :, 0:C], Z2[:, :, C:2 * C], ALU.add).then_inc(s_zs, 1)
                    pool.wait_ge(s_comb, b * COMB + (i + 1) * 2 * NDVE)
                    pool.wait_ge(s_zs, n + 2)
                    part = X[:, 2 * i:2 * i + 2, :]
                    nc.gpsimd.tensor_tensor(part, part, Z2[:, :, 0:C], ALU.add).then_inc(s_zs, 1)

        @block.scalar
        def _(act):
            act.sem_inc(s_pvc, 1)
            with act.Fori(0, batches) as b:
                act.wait_ge(s_xT, b * NCH + 1)
                nc.scalar.activation(XT[:, 0:CH], BK[0], ACT.Copy).then_inc(s_raw0, 1)
                act.wait_ge(s_gn, b + 1)
                for c in range(1, NCH, 2):
                    nc.scalar.activation(XT[:, c * CH:(c + 1) * CH], BK[c], ACT.Identity,
                                         bias=SMALL[:, 4:5], scale=SMALL[:, 3:4]).then_inc(s_xn_act, 1)
                for i in range(2 * NCH):
                    c = i % NCH
                    act.wait_ge(s_proj, b * (3 * NCH) + i + 1)
                    raw = KL if i < NCH else QL
                    nc.scalar.activation(raw[:, c * CH:(c + 1) * CH], BK[c], ACT.Copy)
                    nc.scalar.activation(BK[c], BK[c], ACT.Square,
                                         accum_out=SS[:, i // NCH, c:c + 1]).then_inc(s_sq, 1)
                for c in range(NCH):
                    act.wait_ge(s_proj, b * (3 * NCH) + 2 * NCH + c + 1)
                    nc.scalar.activation(V[:, c * TPB:(c + 1) * TPB, :].rearrange("p t c -> p (t c)"), BK[c],
                                         ACT.Copy).then_inc(s_v, 1)
                act.wait_ge(s_kn, b + 1)
                nc.scalar.activation(QH[:, CH:N].bitcast(F32R), QL[:, CH:N], ACT.Copy,
                                     scale=SMALL[:, 7:8]).then_inc(s_qh, 1)
                act.wait_ge(s_k_in, b * 256 + 256)
                def copy_out(after):
                    act.wait_ge(s_pv, after * T + RING // 2)
                    act.wait_ge(s_ot, after)
                    nc.scalar.activation(PVC[:, :], PV, ACT.Copy).then_inc(s_pvc, 1)

                with act.Fori(0, NCH) as c:
                    for s in range(STEPS):
                        jt, p = s // 2, s % 2
                        if s == 1:
                            with act.If(c):
                                copy_out(b * NCH + c)
                        if p == 0:
                            act.wait_ge(s_pv, b * (NCH * T) + c * T + jt + 1)
                            act.wait_ge(s_adds, b * (NCH * ADDS) + c * ADDS + ADDS0 + adds_until(jt - RING // 2))
                        if s == 0 or s >= AHEAD:
                            act.wait_ge(s_scores, b * SCORED + c * STEPS + max(s + 1, AHEAD))
                        nc.scalar.activation(E[:, s % RING, :], S[s % AHEAD].rearrange("p a n -> p (a n)"), ACT.Exp,
                                             scale=SCALE0).then_inc(s_exp, 1)
                copy_out(b * NCH + NCH)
                def normed(done, half):
                    act.wait_ge(s_ln, b * 4 + 2 * done + half + 1)
                    chunks = range(half * HCH, (half + 1) * HCH)
                    for c in chunks[1::2]:
                        for t in range(c * TPB, (c + 1) * TPB):
                            last = nc.scalar.activation(QL[:, t * C:(t + 1) * C], X[:, t, :], ACT.Identity,
                                                        bias=NM[:, t:t + 1], scale=RY[:, t:t + 1])
                        last.then_inc(s_z_a, 1)
                    for c in chunks:
                        act.wait_ge(s_zT, b * (2 * NCH) + done * NCH + c + 1)
                        nc.scalar.activation(XT[:, c * CH:(c + 1) * CH], BK[c], ACT.Copy).then_inc(s_zc, 1)

                def keys(c):
                    act.wait_ge(s_k1, b * NCH + c + 1)
                    nc.scalar.activation(KH[:, c * CH:(c + 1) * CH], BK[c], ACT.Copy).then_inc(s_k1c, 1)

                def values1(c):
                    act.wait_ge(s_v1, b * NCH + c + 1)
                    nc.scalar.activation(V[:, c * TPB:(c + 1) * TPB, :].rearrange("p t c -> p (t c)"), BK[c],
                                         ACT.Copy).then_inc(s_v1c, 1)

                for half in range(2):
                    chunks = range(half * HCH, (half + 1) * HCH)
                    normed(0, half)
                    for c in chunks:
                        keys(c)
                    if half == 0:
                        for c in chunks:
                            values1(c)
                act.wait_ge(s_k1x, b + 1)
                nc.scalar.activation(KH[:, :], KH[:, :], ACT.Exp, bias=SMALL[:, 8:9],
                                     accum_out=SMALL[:, 9:10]).then_inc(s_k1e, 1)
                for c in range(HCH, NCH):
                    values1(c)
                for c in range(NCH):
                    act.wait_ge(s_kT, b * NCH + c + 1)
                    nc.scalar.activation(KL[:, c * CH:(c + 1) * CH], BK[c], ACT.Copy).then_inc(s_kTc, 1)
                for c in range(NCH):
                    act.wait_ge(s_q1s, b * NCH + c + 1)
                    nc.scalar.activation(QE[:, c * CH:(c + 1) * CH], QE[:, c * CH:(c + 1) * CH],
                                         ACT.Exp).then_inc(s_q1e, 1)
                for i, c in enumerate(q_order):
                    act.wait_ge(s_qT, b * NCH + i + 1)
                    nc.scalar.activation(QT[:, c * CH:(c + 1) * CH], BK[c], ACT.Copy).then_inc(s_qTc, 1)
                normed(1, 0)
                normed(1, 1)
                for half in range(2):
                    pr = PR[:, half * HALF:(half + 1) * HALF, :]
                    act.wait_ge(s_rt, b * 2 + half + 1)
                    nc.scalar.activation(pr, pr, ACT.Exp).then_inc(s_rte, 1)
                for t in range(T):
                    if t % HALF == 0:
                        act.wait_ge(s_gate, b * 2 + t // HALF + 1)
                    if t % 2 == 0 and t >= 4:
                        act.wait_ge(s_zs, b * PAIRS + 3 * (t // 2 - 2) + 1)
                    act.wait_ge(s_ex, b * T + t + 1)
                    for e in range(NDVE, EXPERTS):
                        k = slice((e - NDVE) * C, (e - NDVE + 1) * C)
                        last = nc.scalar.activation(ZX[:, t // 2 % 2, t % 2, k], expert_bank(t, 1)[:, k], ACT.Copy,
                                                    scale=GT[:, t, e:e + 1])
                    last.then_inc(s_zx, 1)

        @block.vector
        def _(dve):
            v = nc.vector

            def chain(done, before):
                n = [0]

                def link(instruction):
                    n[0] += 1
                    instruction.then_inc(done, 1)
                    dve.wait_ge(done, before + n[0])

                return link, n

            def rsqrt(link, y, a, n):
                t, u = RT[:, 0:n], RU[:, 0:n]
                link(v.tensor_scalar(t.bitcast(U32), a.bitcast(U32), 1, None, ALU.logical_shift_right))
                link(v.tensor_scalar(y.bitcast(I32), t.bitcast(I32), -1.0, float(MAGIC), ALU.mult, ALU.add))
                for _ in range(3):
                    link(v.tensor_tensor(u, y, y, ALU.mult))
                    link(v.scalar_tensor_tensor(u, u, -0.5, a, ALU.mult, ALU.mult))
                    link(v.scalar_tensor_tensor(y, u, 1.5, y, ALU.add, ALU.mult))

            def statistics(c):
                for t in range(c * TPB, (c + 1) * TPB):
                    last = v.bn_stats(ST[:, t, :], X[:, t, :])
                return last

            def layernorm(mix_link, half, last):
                mix_link(last)
                tiles = slice(half * HALF, (half + 1) * HALF)
                me, qe, mo, qo = (ST[:, tiles, i] for i in (1, 2, 4, 5))
                mean, ra, rt, ru = MEAN[:, tiles], RA[:, 0:HALF], RT[:, 0:HALF], RU[:, 0:HALF]
                v.tensor_tensor(mean, me, mo, ALU.add)
                v.tensor_tensor(ru, qe, qo, ALU.add)
                mix_link(v.tensor_tensor(ra, me, mo, ALU.subtract))
                v.tensor_scalar(mean, mean, 0.5, None, ALU.mult)
                v.tensor_scalar(ru, ru, 1.0 / C, 1e-5, ALU.mult, ALU.add)
                mix_link(v.tensor_tensor(rt, ra, ra, ALU.mult))
                mix_link(v.scalar_tensor_tensor(ra, rt, 0.25, ru, ALU.mult, ALU.add))
                rsqrt(mix_link, RY[:, tiles], ra, HALF)
                v.scalar_tensor_tensor(NM[:, tiles], mean, -1.0, RY[:, tiles], ALU.mult, ALU.mult).then_inc(s_ln, 1)
                for c in range(half * HCH, (half + 1) * HCH, 2):
                    for t in range(c * TPB, (c + 1) * TPB):
                        last = v.tensor_scalar(QL[:, t * C:(t + 1) * C], X[:, t, :], MEAN[:, t:t + 1], RY[:, t:t + 1],
                                               ALU.subtract, ALU.mult)
                    last.then_inc(s_z_d, 1)

            dve.sem_inc(s_adds, ADDS0)
            dve.sem_inc(s_ot, 1)
            dve.sem_inc(s_rec, 1)
            dve.sem_inc(s_gmax, 1)
            dve.wait_ge(s_const, 12 * 16)
            with dve.Fori(0, batches) as b:
                pre_link, pre_n = chain(s_pre, b * PRE_LINKS)
                for c in (*range(1, NCH), 0):
                    if c:
                        dve.wait_ge(s_xT, b * NCH + c + 1)
                    else:
                        dve.wait_ge(s_raw0, b + 1)
                    last = v.bn_stats(ST[:, c, :], BK[c])
                pre_link(last)
                settle(dve)
                v.bn_aggr(MV[:, :], ST[:, 0:NCH, :].rearrange("p a s -> p (a s)")).then_inc(s_cst, 1)
                dve.wait_ge(s_gm, b * 3 + 1)
                pre_link(v.tensor_copy(SMALL[:, 0:1], BK[0][:, 0:1]))
                pre_link(v.tensor_tensor(SMALL[:, 1:2], MV[:, 0:1], SMALL[:, 0:1], ALU.subtract))
                v.scalar_tensor_tensor(SMALL[:, 2:3], SMALL[:, 1:2], SMALL[:, 1:2], MV[:, 1:2],
                                       ALU.mult, ALU.add).then_inc(s_cst, 1)
                dve.wait_ge(s_gm, b * 3 + 2)
                pre_link(v.tensor_scalar(RA[:, 0:1], BK[0][:, 1:2], 1e-5, None, ALU.add))
                rsqrt(pre_link, SMALL[:, 3:4], RA[:, 0:1], 1)
                v.scalar_tensor_tensor(SMALL[:, 4:5], SMALL[:, 0:1], -1.0, SMALL[:, 3:4],
                                       ALU.mult, ALU.mult).then_inc(s_gn, 1)
                for c in range(0, NCH, 2):
                    v.tensor_scalar(XT[:, c * CH:(c + 1) * CH], XT[:, 0:CH] if c == 0 else BK[c],
                                    SMALL[:, 0:1], SMALL[:, 3:4], ALU.subtract, ALU.mult).then_inc(s_xn_dve, 1)

                for m in range(2):
                    for c in range(NCH):
                        dve.wait_ge(s_sq, b * (2 * NCH) + m * NCH + c + 1)
                        v.reduce_max(MXS[:, m, c:c + 1], BK[c], X_AX).then_inc(s_sqmax, 1)
                    pre_link(v.reduce_sum(RA[:, 1:2], SS[:, m, :], X_AX))
                    pre_link(v.tensor_scalar(RA[:, 0:1], RA[:, 1:2], 1e-24, None, ALU.max))
                    rsqrt(pre_link, SMALL[:, 6 + m:7 + m], RA[:, 0:1], 1)
                    if m == 0:
                        v.tensor_scalar(KH.bitcast(F32R), KL, SMALL[:, 6:7], None, ALU.mult).then_inc(s_kh, 1)
                        dve.wait_ge(s_kh, b * 4 + 1)
                        v.scalar_tensor_tensor(KL.bitcast(F32R), KL, SMALL[:, 6:7], KH,
                                               ALU.mult, ALU.subtract).then_inc(s_kh, 1)
                    else:
                        dve.wait_ge(s_sqmax, b * (2 * NCH) + 2 * NCH)
                        pre_link(v.reduce_max(SMALL[:, 10:12], MXS[:, :, :], X_AX))
                        pre_link(v.tensor_tensor(SMALL[:, 12:14], SMALL[:, 6:8], SMALL[:, 6:8], ALU.mult))
                        pre_link(v.tensor_tensor(SMALL[:, 12:14], SMALL[:, 12:14], SMALL[:, 10:12], ALU.mult))
                        v.reduce_sum(SMALL[:, 14:15], SMALL[:, 12:14], X_AX).then_inc(s_kn, 1)
                        first, others = slice(0, CH), slice(CH, N)
                        pre_link(v.tensor_scalar(QH[:, first].bitcast(F32R), QL[:, first], SMALL[:, 7:8], None, ALU.mult))
                        v.scalar_tensor_tensor(QL[:, first].bitcast(F32R), QL[:, first], SMALL[:, 7:8], QH[:, first],
                                               ALU.mult, ALU.subtract).then_inc(s_kh, 1)
                        dve.wait_ge(s_qh, b + 1)
                        v.scalar_tensor_tensor(QL[:, others].bitcast(F32R), QL[:, others], SMALL[:, 7:8],
                                               QH[:, others], ALU.mult, ALU.subtract).then_inc(s_kh, 1)
                dve.wait_ge(s_gm, b * 3 + 3)
                v.tensor_scalar(FLAG[:, :], BK[0][:, 0:1], 2.0 * safe_bound / SCALE0, None,
                                ALU.is_gt).then_inc(s_flag, 1)
                dve.wait_ge(s_flag, b + 1)
                assert pre_n[0] == PRE_LINKS, pre_n

                def maxima(first):
                    for s in range(STEPS):
                        jt, p = s // 2, s % 2
                        dve.wait_ge(s_gscore, first + (s + 1))
                        rm = RM[:, 2 * p:2 * p + 2, :]
                        if jt == 0:
                            v.tensor_copy(rm, GS).then_inc(s_gmax, 1)
                        else:
                            dve.wait_ge(s_gmax, first + s)
                            v.tensor_tensor(rm, GS, rm, ALU.max).then_inc(s_gmax, 1)

                def attend(c, safe):
                    chunk = b * NCH + c
                    for g in range(NG):
                        for jt in range(FIRST[g] + 1, END[g]):
                            if jt == NORMALISED:
                                with dve.If(c):
                                    normalise(chunk, c)
                            for p in range(2):
                                acc = ACC[:, g % 2, p, :]
                                if jt == FIRST[g] + 1:
                                    if p == 0:
                                        dve.wait_ge(s_sum, chunk * NG + g + 1)
                                    one = E[:, (2 * jt - 2 + p) % RING, :]
                                else:
                                    one = acc
                                    dve.wait_ge(s_adds, chunk * ADDS + ADDS0 + 2 * (jt - g - 1) + p - 1)
                                dve.wait_ge(s_exp, chunk * STEPS + 2 * jt + p + 1)
                                v.tensor_tensor(acc, one, E[:, (2 * jt + p) % RING, :], ALU.add).then_inc(s_adds, 1)
                    if not safe:
                        maxima(b * GEN + c * STEPS + STEPS)

                def normalise(after, place):
                    dve.wait_ge(s_sum, after * NG + 2)
                    v.reciprocal(REC[:, :], SM).then_inc(s_rec, 1)
                    dve.wait_ge(s_pvc, after + 1)
                    dve.wait_ge(s_rec, after + 1)
                    v.tensor_tensor(QH[:, bass.ts(place, CH)], PVC[:, :], REC[:, :], ALU.mult).then_inc(s_ot, 1)
                    dve.wait_ge(s_ot, after + 1)
                    settle(dve)

                settle(dve)
                general = dve.value_load(FLAG[0:1, 0:1], min_val=0, max_val=1)
                with dve.If(general):
                    maxima(b * GEN)
                    with dve.Fori(0, NCH) as c:
                        attend(c, False)
                with dve.Else():
                    dve.sem_inc(s_gmax, GEN)
                    with dve.Fori(0, NCH) as c:
                        attend(c, True)

                mix_link, mix_n = chain(s_mix, b * MIX_LINKS)
                dve.wait_ge(s_bias, b * 4 + 4)

                def onto_x(ready, done, c):
                    dve.wait_ge(ready, b * NCH + c + 1)
                    part = X[:, c * TPB:(c + 1) * TPB, :].rearrange("p t c -> p (t c)")
                    v.tensor_tensor(part, BK[c], part, ALU.add).then_inc(done, 1)

                def onto_x_and_normed(ready, done, half):
                    first = half * HCH
                    for c in range(first, first + HCH):
                        onto_x(ready, done, c)
                        if c > first:
                            dve.wait_ge(done, b * NCH + c)
                            statistics(c - 1)
                    dve.wait_ge(done, b * NCH + first + HCH)
                    layernorm(mix_link, half, statistics(first + HCH - 1))

                onto_x_and_normed(s_y0, s_x0, 0)
                normalise(b * NCH + NCH, 0)
                onto_x_and_normed(s_y0, s_x0, 1)

                for c in range(NCH):
                    dve.wait_ge(s_k1c, b * NCH + c + 1)
                    v.reduce_max(MXS[:, 0, c:c + 1], KH[:, c * CH:(c + 1) * CH], X_AX).then_inc(s_k1m, 1)
                dve.wait_ge(s_k1m, b * NCH + NCH)
                mix_link(v.reduce_max(SMALL[:, 10:11], MXS[:, 0, :], X_AX))
                v.tensor_scalar(SMALL[:, 8:9], SMALL[:, 10:11], -1.0, None, ALU.mult).then_inc(s_k1x, 1)
                for c in range(NCH):
                    g = slice(c * TPB * H, (c + 1) * TPB * H)
                    dve.wait_ge(s_q1, b * NCH + c + 1)
                    q = BK[c].rearrange("p (g d) -> p g d", d=D)
                    e = QE[:, c * CH:(c + 1) * CH].rearrange("p (g d) -> p g d", d=D)
                    mix_link(v.reduce_max(QM[:, g], q, X_AX))
                    v.tensor_tensor(e, q, QM[:, g].unsqueeze(2).to_broadcast([P, TPB * H, D]),
                                    ALU.subtract).then_inc(s_q1s, 1)
                for i, c in enumerate(q_order):
                    g = slice(c * TPB * H, (c + 1) * TPB * H)
                    dve.wait_ge(s_q1e, b * NCH + c + 1)
                    mix_link(v.reduce_sum(QSUM[:, g], QE[:, c * CH:(c + 1) * CH].rearrange("p (g d) -> p g d", d=D), X_AX))
                    v.reciprocal(QSUM[:, g], QSUM[:, g]).then_inc(s_q1r, 1)
                    if i == 2:
                        dve.wait_ge(s_k1e, b + 1)
                        mix_link(v.reciprocal(SMALL[:, 11:12], SMALL[:, 9:10]))
                        dve.wait_ge(s_ctx, b * 2 + 1)
                        v.scalar_tensor_tensor(CTX[:, :], BK[0][:, 0:C], SMALL[:, 11:12], BLOCK,
                                               ALU.mult, ALU.mult).then_inc(s_at, 1)
                    if i == 5:
                        dve.wait_ge(s_ctx, b * 2 + 2)
                        v.scalar_tensor_tensor(AT[:, :], BO1[:, :], 1.0 / H, BK[0][:, C:2 * C],
                                               ALU.mult, ALU.add).then_inc(s_at, 1)
                mix_link(v.memset(G32[:, :, :], 0.0))
                for i, c in enumerate(q_order):
                    dve.wait_ge(s_y1, b * NCH + i + 1)
                    last = v.bn_stats(ST[:, c, :], BK[c])
                mix_link(last)
                settle(dve)
                v.bn_aggr(MV[:, :], ST[:, 0:NCH, :].rearrange("p a s -> p (a s)")).then_inc(s_bst, 1)
                dve.wait_ge(s_gst, b * 2 + 1)
                mix_link(v.tensor_copy(SMALL[:, 0:1], BK[0][:, 0:1]))
                mix_link(v.tensor_tensor(SMALL[:, 1:2], MV[:, 0:1], SMALL[:, 0:1], ALU.add))
                v.scalar_tensor_tensor(SMALL[:, 2:3], SMALL[:, 1:2], SMALL[:, 1:2], MV[:, 1:2],
                                       ALU.mult, ALU.add).then_inc(s_bst, 1)
                dve.wait_ge(s_gst, b * 2 + 2)
                mix_link(v.tensor_scalar(RA[:, 0:1], BK[0][:, 1:2], -1.0, 1e-5, ALU.mult, ALU.add))
                rsqrt(mix_link, SMALL[:, 3:4], RA[:, 0:1], 1)
                mix_link(v.tensor_scalar(GA[:, :], GNW[:, :], SMALL[:, 3:4], None, ALU.mult))
                v.scalar_tensor_tensor(GB[:, :], GA[:, :], SMALL[:, 0:1], GNB[:, :], ALU.mult, ALU.add)
                mix_link(v.tensor_tensor(AT2[:, :], AT[:, :], GA[:, :], ALU.mult))
                v.scalar_tensor_tensor(AT2[:, :], GB[:, :], 1.0 / H, AT2[:, :], ALU.mult, ALU.add).then_inc(s_at, 1)

                for half in range(2):
                    onto_x_and_normed(s_y2, s_x1, half)

                def over(x2):
                    return x2.unsqueeze(2).to_broadcast([P, HALF, EXPERTS])

                def rows(x3, half):
                    return x3[:, half * HALF:(half + 1) * HALF]

                def logits(half):
                    l = rows(L, half)
                    bank = BK[7 * half][:, 0:HALF * EXPERTS].rearrange("p (t e) -> p t e", e=EXPERTS)
                    dve.wait_ge(s_route, b * 2 + half + 1)
                    mix_link(v.tensor_tensor(l, bank, RB[:, :].unsqueeze(1).to_broadcast([P, HALF, EXPERTS]), ALU.add))
                    mix_link(v.reduce_max(rows(R1[:, 0, :], half), l, X_AX))
                    v.tensor_tensor(rows(PR, half), l, over(rows(R1[:, 0, :], half)), ALU.subtract).then_inc(s_rt, 1)

                rank = RANK.unsqueeze(1).to_broadcast([P, HALF, EXPERTS])

                def probabilities(half):
                    pr, total = rows(PR, half), rows(R1[:, 1, :], half)
                    dve.wait_ge(s_rte, b * 2 + half + 1)
                    mix_link(v.reduce_sum(total, pr, X_AX))
                    mix_link(v.reciprocal(total, total))
                    mix_link(v.tensor_tensor(pr, pr, over(total), ALU.mult))

                def pick(half, best, onehot):
                    pr, top, best, onehot = (rows(x, half) for x in (PR, R1[:, 0, :], R1[:, best, :], onehot))
                    mix_link(v.reduce_max(best, pr, X_AX))
                    mix_link(v.tensor_tensor(onehot, pr, over(best), ALU.is_equal))
                    mix_link(v.tensor_tensor(onehot, onehot, rank, ALU.mult))
                    mix_link(v.reduce_max(top, onehot, X_AX))
                    mix_link(v.tensor_tensor(onehot, rank, over(top), ALU.is_equal))

                def second(half):
                    pr = rows(PR, half)
                    mix_link(v.scalar_tensor_tensor(pr, rows(OH, half), -2.0, pr, ALU.mult, ALU.add))
                    pick(half, 3, TK)

                def gates(half):
                    total, p1, p2 = (rows(R1[:, i, :], half) for i in (1, 2, 3))
                    oh, tk = rows(OH, half), rows(TK, half)
                    mix_link(v.tensor_tensor(total, p1, p2, ALU.add))
                    mix_link(v.reciprocal(total, total))
                    v.tensor_tensor(p1, p1, total, ALU.mult)
                    mix_link(v.tensor_tensor(p2, p2, total, ALU.mult))
                    v.tensor_tensor(oh, oh, over(p1), ALU.mult)
                    mix_link(v.tensor_tensor(tk, tk, over(p2), ALU.mult))
                    v.tensor_tensor(rows(GT, half), oh, tk, ALU.add)
                    v.tensor_tensor(rows(G32, half)[:, :, 0:EXPERTS], oh, tk, ALU.add).then_inc(s_gate, 1)

                def gates_out(half):
                    dve.wait_ge(s_gtT, b * 2 + half + 1)
                    v.tensor_copy(GTT[:, HCH * half:HCH * (half + 1), :].rearrange("p a n -> p (a n)"),
                                  BK[7 * half]).then_inc(s_gtc, 1)

                def combine(c):
                    part = X[:, c * TPB:(c + 1) * TPB, :].rearrange("p t c -> p (t c)")
                    dve.wait_ge(s_ebm, b * NCH + c + 1)
                    v.tensor_tensor(part, BK[7 * (c // HCH)], part, ALU.add).then_inc(s_eba, 1)
                    dve.wait_ge(s_eba, b * NCH + c + 1)
                    for t in range(c * TPB, (c + 1) * TPB):
                        dve.wait_ge(s_ex, b * T + t + 1)
                        for e in range(NDVE):
                            if e:
                                dve.wait_ge(s_comb, b * COMB + t * NDVE + e)
                            v.scalar_tensor_tensor(X[:, t, :], expert_bank(t, 0)[:, e * C:(e + 1) * C],
                                                   GT[:, t, e:e + 1], X[:, t, :], ALU.mult, ALU.add).then_inc(s_comb, 1)

                logits(0)
                probabilities(0)
                pick(0, 2, OH)
                second(0)
                gates(0)
                logits(1)
                gates_out(0)
                combine(0)
                probabilities(1)
                pick(1, 2, OH)
                combine(1)
                second(1)
                combine(2)
                gates(1)
                gates_out(1)
                combine(3)
                for c in range(HCH, NCH):
                    combine(c)
                assert mix_n[0] == MIX_LINKS, mix_n

        @block.tensor
        def _(pe):
            def mm(o, lhsT, rhs, start=True, stop=True, shared=False):
                return nc.tensor.matmul(o, lhsT, rhs, start=start, stop=stop, skip_group_check=shared)

            def transposes(dst, src, c):
                for t in range(c * TPB, (c + 1) * TPB):
                    last = nc.tensor.transpose(dst[:, (t % TPB) * P:(t % TPB + 1) * P], src(t), IDENT)
                return last

            pe.sem_inc(s_pv, RING // 2)
            pe.sem_inc(s_sum, 2)
            pe.wait_ge(s_const, 12 * 16)
            pe.wait_ge(s_eb, TPB * 16)
            with pe.Fori(0, batches) as b:
                with pe.If(b):
                    pe.wait_ge(s_comb, b * COMB)
                    pe.wait_ge(s_zx, b * T)
                    settle(pe)
                for c in range(NCH):
                    if c % 2 == 0:
                        pe.wait_ge(s_x_in[c // 2], b * 16 + 16)
                    transposes(BK[c], lambda t: XN[:, t, :], c).then_inc(s_xT, 1)
                pe.wait_ge(s_raw0, b + 1)
                pe.wait_ge(s_cst, b * 2 + 1)
                mm(BK[0][:, 0:1], GAVG, MV[:, 0:1]).then_inc(s_gm, 1)
                pe.wait_ge(s_cst, b * 2 + 2)
                mm(BK[0][:, 1:2], GAVG, SMALL[:, 2:3]).then_inc(s_gm, 1)
                for i, m in enumerate((1, 0)):
                    for c in range(NCH):
                        if i == 0:
                            if c % 2:
                                pe.wait_ge(s_xn_act, b * 4 + (c + 1) // 2)
                            else:
                                pe.wait_ge(s_xn_dve, b * 4 + c // 2 + 1)
                        else:
                            pe.wait_ge(s_sqmax, b * (2 * NCH) + c + 1)
                        mm(BK[c], WQKV[:, m * C:(m + 1) * C], XT[:, c * CH:(c + 1) * CH]).then_inc(s_proj, 1)
                for c in range(NCH):
                    pe.wait_ge(s_sqmax, b * (2 * NCH) + NCH + c + 1)
                    for t in range(c * TPB, (c + 1) * TPB):
                        last = mm(BK[c][:, (t % TPB) * C:(t % TPB + 1) * C], XT[:, t * P:(t + 1) * P], WQKV[:, 2 * C:3 * C])
                    last.then_inc(s_proj, 1)
                pe.wait_ge(s_kn, b + 1)
                pe.wait_ge(s_v, b * NCH + NCH)
                mm(BK[0][:, 0:1], ONES, SMALL[:, 14:15]).then_inc(s_gm, 1)
                pe.wait_ge(s_flag, b + 1)

                def scores(s, par, safe):
                    jt, p = s // 2, s % 2
                    for i in range(2):
                        h = 2 * p + i
                        last = mm(S[s % AHEAD][:, i, :], KS[:, h, jt * P:(jt + 1) * P],
                                  QS[:, par, h, :], stop=safe)
                        if not safe:
                            last = mm(S[s % AHEAD][:, i, :], NEG, RM[:, h, :], start=False)
                    return last

                def maxima(par, first, reds):
                    for s in range(STEPS):
                        jt, p = s // 2, s % 2
                        pe.wait_ge(s_gmax, first + (s + 1))
                        for i in range(2):
                            last = mm(GS[:, i, :], KS[:, 2 * p + i, jt * P:(jt + 1) * P], QS[:, par, 2 * p + i, :])
                        last.then_inc(s_gscore, 1)
                    pe.wait_ge(s_gred, reds)

                def values(jt):
                    for h in range(H):
                        e = E[:, (2 * jt + h // 2) % RING, (h % 2) * CH:(h % 2 + 1) * CH]
                        last = mm(PV[D * h:D * h + D, :], V[:, jt, D * h:D * h + D], e, start=(jt == 0), stop=(jt == T - 1))
                    last.then_inc(s_pv, 1)

                def sums(g, adds):
                    pe.wait_ge(s_adds, adds)
                    for h in range(H):
                        a = ACC[:, g % 2, h // 2, (h % 2) * CH:(h % 2 + 1) * CH]
                        last = mm(SM[D * h:D * h + D, :], ONES[:, 0:D], a, start=(g == 0), stop=(g == NG - 1))
                    last.then_inc(s_sum, 1)

                early = [(STEPS - AHEAD + i) % AHEAD for i in range(AHEAD)]

                def attend(c, safe):
                    chunk = b * NCH + c
                    for s in range(STEPS):
                        jt = s // 2
                        pe.wait_ge(s_exp, chunk * STEPS + s + 1)
                        if s == STEPS - AHEAD:
                            pe.wait_ge(s_q_in, b * QLOADS + (c + 2) * 256)
                            if not safe:
                                maxima((c + 1) % 2, b * GEN + c * STEPS + STEPS, b * (NCH + 1) + c + 2)
                        if s < STEPS - AHEAD:
                            last = scores(s + AHEAD, c % 2, safe)
                        else:
                            last = scores(early[s + AHEAD - STEPS], (c + 1) % 2, safe)
                        last.then_inc(s_scores, 1)
                        if s % 2:
                            if jt == 0:
                                pe.wait_ge(s_pvc, chunk + 1)
                            values(jt)
                            if jt == LAG - 1:
                                with pe.If(c):
                                    sums(NG - 1, chunk * ADDS + ADDS0)
                            for g in range(NG - 1):
                                if jt == END[g] - 1 + LAG:
                                    if g == 0:
                                        pe.wait_ge(s_rec, chunk + 1)
                                    sums(g, chunk * ADDS + (ADDS0 + 2 * (END[g] - g - 1)))

                pe.wait_ge(s_k_in, b * 256 + 256)
                pe.wait_ge(s_q_in, b * QLOADS + 256)
                settle(pe)
                general = pe.value_load(FLAG[0:1, 0:1], min_val=0, max_val=1)
                with pe.If(general):
                    maxima(0, b * GEN, b * (NCH + 1) + 1)
                    for s in early:
                        scores(s, 0, False).then_inc(s_scores, 1)
                    with pe.Fori(0, NCH) as c:
                        attend(c, False)
                with pe.Else():
                    pe.sem_inc(s_gscore, GEN)
                    for s in early:
                        scores(s, 0, True).then_inc(s_scores, 1)
                    with pe.Fori(0, NCH) as c:
                        attend(c, True)

                def tiles(lhsT, rhs, signal, before=None, onto=None):
                    for c in range(NCH):
                        if before:
                            before(c)
                        for t in range(c * TPB, (c + 1) * TPB):
                            last = mm(BK[c][:, (t % TPB) * C:(t % TPB + 1) * C], lhsT(t), rhs(t))
                        last.then_inc(signal, 1)

                def project(c):
                    for t in range(c * TPB, (c + 1) * TPB):
                        place = (t + TPB) % T
                        last = mm(BK[c][:, (t % TPB) * C:(t % TPB + 1) * C], QH[:, place * P:(place + 1) * P], WOUT0[:, :])
                    last.then_inc(s_y0, 1)

                pe.wait_ge(s_ot, b * NCH + NCH)
                for c in range(3):
                    project(c)
                project(3)
                sums(NG - 1, (b * NCH + NCH) * ADDS + ADDS0)
                project(4)
                project(5)
                pe.wait_ge(s_pvc, b * NCH + NCH + 1)
                project(6)

                def transposed(done, c):
                    if c % 2:
                        pe.wait_ge(s_z_a, b * NCH + done * (NCH // 2) + c // 2 + 1)
                    else:
                        pe.wait_ge(s_z_d, b * NCH + done * (NCH // 2) + c // 2 + 1)
                    transposes(BK[c], lambda t: QL[:, t * C:(t + 1) * C], c).then_inc(s_zT, 1)

                def token_major(c, weights, signal):
                    for t in range(c * TPB, (c + 1) * TPB):
                        last = mm(BK[c][:, (t % TPB) * C:(t % TPB + 1) * C], XT[:, t * P:(t + 1) * P], weights)
                    last.then_inc(signal, 1)

                for half in range(2):
                    chunks = range(half * HCH, (half + 1) * HCH)
                    for c in chunks:
                        transposed(0, c)
                    for c in chunks:
                        pe.wait_ge(s_zc, b * (2 * NCH) + c + 1)
                        mm(BK[c], WQKV1[:, C:2 * C], XT[:, c * CH:(c + 1) * CH]).then_inc(s_k1, 1)
                    if half == 0:
                        pe.wait_ge(s_ot, b * NCH + NCH + 1)
                        project(7)
                    for c in chunks:
                        pe.wait_ge(s_k1c, b * NCH + c + 1)
                        token_major(c, WQKV1[:, 2 * C:3 * C], s_v1)
                pe.wait_ge(s_k1e, b + 1)
                for c in range(NCH):
                    pe.wait_ge(s_v1c, b * NCH + c + 1)
                    transposes(BK[c], lambda t: KH[:, t * P:(t + 1) * P], c).then_inc(s_kT, 1)
                for c in range(NCH):
                    pe.wait_ge(s_kTc, b * NCH + c + 1)
                    token_major(c, WQKV1[:, 0:C], s_q1)
                pe.wait_ge(s_q1s, b * NCH + 1)
                for t in range(T):
                    last = mm(BK[0][:, 0:C], KL[:, t * P:(t + 1) * P], V[:, t, :], start=(t == 0), stop=(t == T - 1))
                last.then_inc(s_ctx, 1)
                for i, c in enumerate(q_order):
                    if i == 4:
                        pe.wait_ge(s_at, b * 3 + 1)
                        mm(BK[0][:, C:2 * C], CTX[:, :], WOUT1[:, :]).then_inc(s_ctx, 1)
                    if c == 0:
                        pe.wait_ge(s_at, b * 3 + 2)
                    pe.wait_ge(s_q1n, b * NCH + i + 1)
                    transposes(BK[c], lambda t: QE[:, t * P:(t + 1) * P], c).then_inc(s_qT, 1)
                for i, c in enumerate(q_order):
                    pe.wait_ge(s_qTc, b * NCH + i + 1)
                    for t in range(c * TPB, (c + 1) * TPB):
                        last = mm(BK[c][:, (t % TPB) * C:(t % TPB + 1) * C], QT[:, t * P:(t + 1) * P], AT[:, :])
                    last.then_inc(s_y1, 1)
                pe.wait_ge(s_bst, b * 2 + 1)
                mm(BK[0][:, 0:1], NEG, MV[:, 0:1]).then_inc(s_gst, 1)
                pe.wait_ge(s_bst, b * 2 + 2)
                mm(BK[0][:, 1:2], NEG, SMALL[:, 2:3]).then_inc(s_gst, 1)
                pe.wait_ge(s_at, b * 3 + 3)
                tiles(lambda t: QT[:, t * P:(t + 1) * P], lambda t: AT2[:, :], s_y2)

                for half in range(2):
                    for c in range(half * HCH, (half + 1) * HCH):
                        transposed(1, c)
                    pe.wait_ge(s_zc, b * (2 * NCH) + NCH + (half + 1) * HCH)
                    for i in range(HALF):
                        t = half * HALF + i
                        last = mm(BK[7 * half][:, i * EXPERTS:(i + 1) * EXPERTS], XT[:, t * P:(t + 1) * P], WR[:, :])
                    last.then_inc(s_route, 1)

                def gates(half):
                    pe.wait_ge(s_gate, b * 2 + half + 1)
                    for k in range(HCH):
                        a = HCH * half + k
                        last = nc.tensor.transpose(BK[7 * half][:, k * P:(k + 1) * P],
                                                   G32[:, TPB * a:TPB * (a + 1), :].rearrange("p t e -> p (t e)"), IDENT)
                    last.then_inc(s_gtT, 1)

                def biases(c):
                    if c % HCH == 0:
                        pe.wait_ge(s_gtc, b * 2 + c // HCH + 1)
                    else:
                        pe.wait_ge(s_eba, b * NCH + c)
                    for t in range(TPB):
                        last = mm(BK[7 * (c // HCH)][:, t * C:(t + 1) * C], GTT[:, c, :], EB[:, t, :])
                    last.then_inc(s_ebm, 1)

                gates(0)
                for t in range(T):
                    if t == 1:
                        biases(0)
                    if t == HALF - TPB + 1:
                        gates(1)
                    if t % TPB == 0 and t:
                        biases(t // TPB)
                    if t >= EBUF:
                        pe.wait_ge(s_comb, b * COMB + (t - EBUF + 1) * NDVE)
                        pe.wait_ge(s_zx, b * T + t - EBUF + 1)
                    for part in range(2):
                        last = mm(expert_bank(t, part), XT[:, t * P:(t + 1) * P],
                                  WEXP[:, part * NDVE:(part + 1) * NDVE, :].rearrange("p e c -> p (e c)"))
                    last.then_inc(s_ex, 1)


_INS = ["x", "L0_conv_w_qkv", "L0_conv_w_out", "L0_conv_b_out", "L1_attn_W_qkv", "L1_attn_W_out", "L1_attn_b_out",
        "L1_attn_gn_w", "L1_attn_gn_b", "L1_ffn_router_w", "L1_ffn_router_b", "L1_ffn_expert_w", "L1_ffn_expert_b"]


def constants():
    i = np.arange(P)
    per = C // G
    rank = np.zeros((P, P))
    rank[:, 0:EXPERTS] = EXPERTS - np.arange(EXPERTS)
    return np.concatenate([
        np.eye(P), (i[:, None] // per == i[None, :] // per) / per, np.ones((P, P)), np.full((P, P), -1.0 / P),
        (i[:, None] // D == i[None, :] // D) * SCALE1, rank], axis=1).astype(np.float32)


def kernel(**inputs):
    import concourse.bacc as bacc
    from concourse.bass_utils import run_bass_kernel_spmd

    nc = bacc.Bacc("TRN2", target_bir_lowering=False, num_devices=1, dynamic_dma_scratch_size=1024)
    given = {n: np.asarray(inputs[n]) for n in _INS}
    for n in ("L1_attn_W_qkv", "L1_attn_W_out"):
        given[n] = given[n].T
    given["consts"] = constants()
    arrays, args = {}, []
    for n, a in given.items():
        arrays[f"in_{n}"] = np.ascontiguousarray(a)
        args.append(nc.dram_tensor(f"in_{n}", a.shape, mybir.dt.from_np(a.dtype), kind="ExternalInput").ap())
    args.append(nc.dram_tensor("out_0", (B, 64, 64, C), F32, kind="ExternalOutput").ap())
    hybrid_kernel(nc, *args)
    r = run_bass_kernel_spmd(nc, [arrays], core_ids=[0])
    return np.asarray(r.results[0]["out_0"])
```

```python
import numpy as np
import concourse.bass as bass
from concourse import mybir
from contextlib import ExitStack

F32 = mybir.dt.float32
F32R = mybir.dt.float32r
U32 = mybir.dt.uint32
I32 = mybir.dt.int32
ALU = mybir.AluOpType
ACT = mybir.ActivationFunctionType
X_AX = mybir.AxisListType.X

P = 128
B = 4
N = 64 * 64
C = 128
T = N // P
H = 4
D = C // H
CH = 512
NCH = N // CH
TPB = CH // P
G = 32
EXPERTS = 8
SCALE0 = 10.0
SCALE1 = D ** -0.5
SAFE_BOUND = 40.0
MAGIC = 0x5F3759DF

STEPS = 2 * T
AHEAD = 3
SCORED = STEPS * NCH + AHEAD
RING = 8
GROUPS = (6, 6, 6, 7, 7)
NG = len(GROUPS)
FIRST = [sum(GROUPS[:g]) for g in range(NG)]
END = [sum(GROUPS[:g + 1]) for g in range(NG)]
ADDS = 2 * (T - NG)
ADDS0 = 2 * (GROUPS[-1] - 1)
LAG = 3
NORMALISED = 5
QLOADS = (NCH + 1) * 16 * 4 * H
GEN = STEPS * (NCH + 1)



def buffer(t):
    return (AHEAD - 2) if t % STEPS == STEPS - 1 else t % STEPS % AHEAD


def scored_after(s):
    at = [max(max(w for w in range(u) if buffer(w) == buffer(u)) for u in range(AHEAD, t + 1))
          for t in range(AHEAD, STEPS + AHEAD)]
    return [AHEAD + i for i, a in enumerate(at) if a == s]


def adds_until(j):
    if j < 0:
        return adds_until(T + j) - ADDS
    g = max(g for g in range(NG) if FIRST[g] <= j)
    return 2 * (FIRST[g] - g + max(j - FIRST[g], 1))


HALF = T // 2
HCH = NCH // 2
NDVE = EXPERTS // 2
EBUF = 3

UNITS = NCH * H
ACT_UNITS = 20
KS_ACT = ACT_UNITS + H // 2
KS_DVE = UNITS - ACT_UNITS + H // 2

PRE_LINKS = 45
MIX_LINKS = 137


def hybrid_kernel(nc, x, w_qkv0, w_out0, b_out0, w_qkvT, w_outT, b_out1, gn_w, gn_b, router_w, router_b,
                  expert_w, expert_b, consts, out, safe_bound=SAFE_BOUND, batches=B):
    x_v = x.rearrange("b y z c -> (b y z c)").rearrange("(b p n) -> b p n", b=B, p=P)
    out_v = out.rearrange("b y z c -> (b y z c)").rearrange("(b p n) -> b p n", b=B, p=P)

    ctx = ExitStack()
    with ctx:
        def sb(name, shape, dt=F32, stack=ctx):
            return stack.enter_context(nc.sbuf_tensor(name, shape, dt))

        def sem(name):
            return ctx.enter_context(nc.semaphore(name))

        def settle(engine):
            engine.sem_inc(s_settled, 1)

        X = sb("X", [P, T, C])
        XT = sb("XT", [P, N])
        parts = ExitStack()
        QP = sb("QP", [P, 2 * N], F32R, parts)
        parts.close()
        QH = sb("QH", [P, N])
        QL = sb("QL", [P, N])
        parts = ExitStack()
        KP = sb("KP", [P, 2 * N], F32R, parts)
        parts.close()
        KE = sb("KE", [P, 2 * N])
        V = sb("V", [P, T, C])
        KH, KL = KE[:, 0:N], KE[:, N:2 * N]
        KPH, KPL = KP[:, 0:N], KP[:, N:2 * N]
        QPH, QPL = QP[:, 0:N], QP[:, N:2 * N]
        E = KE[:, :].rearrange("p (r n) -> p r n", r=RING)
        ACC = XT[:, :].rearrange("p (g s n) -> p g s n", g=2, s=2)

        WQKV = sb("WQKV", [P, 3 * C])
        WOUT0 = sb("WOUT0", [P, C])
        WQKV1 = sb("WQKV1", [P, 3 * C])
        WOUT1 = sb("WOUT1", [P, C])
        WEXP = sb("WEXP", [P, EXPERTS, C])
        WR = sb("WR", [P, EXPERTS])
        RB = sb("RB", [P, EXPERTS])
        BO0 = sb("BO0", [P, C])
        BO1 = sb("BO1", [P, C])
        GNW = sb("GNW", [P, C])
        GNB = sb("GNB", [P, C])
        EB = sb("EB", [P, TPB, C])
        CONST = sb("CONST", [P, 6 * P])
        IDENT = CONST[:, 0:P]
        GAVG = CONST[:, P:2 * P]
        ONES = CONST[:, 2 * P:3 * P]
        NEG = CONST[:, 3 * P:4 * P]
        BLOCK = CONST[:, 4 * P:5 * P]
        RANK = CONST[:, 5 * P:5 * P + EXPERTS]

        ST = sb("ST", [P, T, 6])
        MV = sb("MV", [P, 2])
        SMALL = sb("SMALL", [P, 16])
        KSUM = sb("KSUM", [P, 2])
        SS = sb("SS", [P, 2, NCH])
        MXS = sb("MXS", [P, 2, NCH])
        RT = sb("RT", [P, T])
        RU = sb("RU", [P, T])
        RA = sb("RA", [P, T])
        RY = sb("RY", [P, T])
        MEAN = sb("MEAN", [P, T])
        FLAG = sb("FLAG", [P, 1], I32)
        PVC = sb("PVC", [P, CH])
        REC = sb("REC", [P, CH])

        attn = ExitStack()
        KS = sb("KS", [P, H, N], F32R, attn)
        load = ExitStack()
        QSF = sb("QSF", [P, 2, H, CH], F32, load)
        load.close()
        QS = sb("QS", [P, 2, H, CH], F32R, attn)
        PICK, PICKF = (t[:, 1, :, :].rearrange("p h n -> p (h n)") for t in (QS, QSF))
        RM = sb("RM", [P, H, CH], F32, attn)
        attn.close()
        mix = ExitStack()
        QE = sb("QE", [P, N], F32, mix)
        QT = sb("QT", [P, N], F32, mix)
        XN = sb("XN", [P, T, C], F32, mix)
        ZX = sb("ZX", [P, 2, 2, NDVE * C], F32, mix)
        Z2 = sb("Z2", [P, 2, 2 * C], F32, mix)
        NM = sb("NM", [P, T], F32, mix)
        QM = sb("QM", [P, T * H], F32, mix)
        QSUM = sb("QSUM", [P, T * H], F32, mix)
        CTX = sb("CTX", [P, C], F32, mix)
        AT = sb("AT", [P, C], F32, mix)
        AT2 = sb("AT2", [P, C], F32, mix)
        GA = sb("GA", [P, C], F32, mix)
        GB = sb("GB", [P, C], F32, mix)
        L = sb("L", [P, T, EXPERTS], F32, mix)
        PR = sb("PR", [P, T, EXPERTS], F32, mix)
        OH = sb("OH", [P, T, EXPERTS], F32, mix)
        TK = sb("TK", [P, T, EXPERTS], F32, mix)
        GT = sb("GT", [P, T, EXPERTS], F32, mix)
        G32 = sb("G32", [P, T, 32], F32, mix)
        GTT = sb("GTT", [P, NCH, P], F32, mix)
        R1 = sb("R1", [P, 4, T], F32, mix)
        mix.close()

        BK8 = ctx.enter_context(nc.psum_tensor("BK8", [P, 8, CH], F32))
        BK = [BK8[:, i, :] for i in range(8)]
        S = [BK8[:, 2 * i:2 * i + 2, :] for i in range(AHEAD)]
        PV, SM = BK[2 * AHEAD], BK[2 * AHEAD + 1]
        GS = S[buffer(STEPS)]

        s_settled = sem("s_settled")
        s_const = sem("s_const")
        s_x_in = [sem(f"s_x_in{i}") for i in range(4)]
        s_x_out = [sem(f"s_x_out{i}") for i in range(4)]
        s_eb0 = sem("s_eb0")
        s_eb = sem("s_eb")
        s_start = sem("s_start")
        s_xT = sem("s_xT")
        s_raw0 = sem("s_raw0")
        s_pre = sem("s_pre")
        s_cst = sem("s_cst")
        s_gm = sem("s_gm")
        s_gn = sem("s_gn")
        s_xn_act = sem("s_xn_act")
        s_xn_dve = sem("s_xn_dve")
        s_proj = sem("s_proj")
        s_sq = sem("s_sq")
        s_sqmax = sem("s_sqmax")
        s_kn = sem("s_kn")
        s_qh = sem("s_qh")
        s_kh = sem("s_kh")
        s_v = sem("s_v")
        s_flag = sem("s_flag")
        s_bias = sem("s_bias")
        s_pick = sem("s_pick")
        s_picked = sem("s_picked")
        s_stack = sem("s_stack")
        s_ks_act = sem("s_ks_act")
        s_ks_dve = sem("s_ks_dve")
        s_q_in = sem("s_q_in")
        s_scores = sem("s_scores")
        s_exp = sem("s_exp")
        s_pv = sem("s_pv")
        s_adds = sem("s_adds")
        s_sum = sem("s_sum")
        s_pvc = sem("s_pvc")
        s_rec = sem("s_rec")
        s_ot = sem("s_ot")
        s_gscore = sem("s_gscore")
        s_gmax = sem("s_gmax")
        s_gred = sem("s_gred")
        s_y0 = sem("s_y0")
        s_mix = sem("s_mix")
        s_x0 = sem("s_x0")
        s_x1 = sem("s_x1")
        s_ln = sem("s_ln")
        s_z_d = sem("s_z_d")
        s_z_a = sem("s_z_a")
        s_zT = sem("s_zT")
        s_zc = sem("s_zc")
        s_k1 = sem("s_k1")
        s_k1c = sem("s_k1c")
        s_k1m = sem("s_k1m")
        s_k1x = sem("s_k1x")
        s_k1e = sem("s_k1e")
        s_v1 = sem("s_v1")
        s_v1c = sem("s_v1c")
        s_q1 = sem("s_q1")
        s_q1s = sem("s_q1s")
        s_q1e = sem("s_q1e")
        s_q1r = sem("s_q1r")
        s_q1n = sem("s_q1n")
        s_kT = sem("s_kT")
        s_kTc = sem("s_kTc")
        s_ctx = sem("s_ctx")
        s_at = sem("s_at")
        s_qT = sem("s_qT")
        s_qTc = sem("s_qTc")
        s_y1 = sem("s_y1")
        s_y2 = sem("s_y2")
        s_bst = sem("s_bst")
        s_gst = sem("s_gst")
        s_route = sem("s_route")
        s_rt = sem("s_rt")
        s_rte = sem("s_rte")
        s_gate = sem("s_gate")
        s_gtT = sem("s_gtT")
        s_gtc = sem("s_gtc")
        s_ebm = sem("s_ebm")
        s_eba = sem("s_eba")
        s_ex = sem("s_ex")
        s_comb = sem("s_comb")
        s_zx = sem("s_zx")
        s_zs = sem("s_zs")

        COMB = T * NDVE
        PAIRS = T // 2 * 3

        def expert_bank(t, part):
            return BK[1 + 2 * (t % EBUF) + part]

        def stacked(u):
            return KS[:, u % H, u // H * CH:(u // H + 1) * CH]

        k_order = (*range(HCH, NCH), *range(HCH))
        q_order = (*range(1, NCH), 0)

        block = ctx.enter_context(nc.Block())

        @block.sync
        def _(sp):
            loads = [(WQKV[:, :], w_qkv0), (WOUT0[:, :], w_out0), (WQKV1[:, :], w_qkvT), (WOUT1[:, :], w_outT),
                     (WEXP[:, :, :], expert_w.rearrange("e d c -> d e c")), (WR[:, :], router_w),
                     (RB[:, :], router_b.partition_broadcast(P)), (BO0[:, :], b_out0.partition_broadcast(P)),
                     (BO1[:, :], b_out1.partition_broadcast(P)), (GNW[:, :], gn_w.partition_broadcast(P)),
                     (GNB[:, :], gn_b.partition_broadcast(P)), (CONST[:, :], consts[:, 0:6 * P])]
            for dst, src in loads:
                sp.dma_start(dst, src).then_inc(s_const, 16)
            sp.wait_ge(s_eb0, 1)
            for s in range(TPB):
                sp.dma_start(EB[32 * s:32 * s + EXPERTS, s, :], expert_b).then_inc(s_eb, 16)

            def load_x(b):
                for i in range(4):
                    part = slice(i * T // 4 * C, (i + 1) * T // 4 * C)
                    sp.dma_start(XN[:, :, :].rearrange("p t c -> p (t c)")[:, part], x_v[b, :, part]).then_inc(s_x_in[i], 16)

            def stack(b):
                sp.wait_ge(s_bias, b * 4 + 4)
                settle(sp)
                sp.dma_start(PICKF, consts[:, 6 * P:(6 + 4 * H) * P]).then_inc(s_pick, 16)
                def load_q(c):
                    for r in range(4):
                        for h in range(H):
                            src = (QPH if r % 2 == 0 else QPL).bitcast(F32)
                            sp.dma_start(QS[D * r:D * r + D, c % 2, h, :].bitcast(F32),
                                         src[D * h:D * h + D, bass.ts(c, CH)]).then_inc(s_q_in, 16)

                sp.sem_inc(s_q_in, 256)
                sp.wait_ge(s_kh, b * 5 + 5)
                load_q(1)
                with sp.Fori(2, NCH) as c:
                    sp.wait_ge(s_q_in, b * QLOADS + c * 256)
                    sp.wait_ge(s_scores, b * SCORED + (c * STEPS - STEPS))
                    load_q(c)
                sp.wait_ge(s_q_in, b * QLOADS + NCH * 256)
                sp.sem_inc(s_q_in, 256)

            def store(b):
                for i in range(4):
                    part = slice(i * T // 4 * C, (i + 1) * T // 4 * C)
                    sp.wait_ge(s_zs, b * PAIRS + (i + 1) * PAIRS // 4)
                    sp.dma_start(out_v[b, :, part], X[:, :, :].rearrange("p t c -> p (t c)")[:, part]).then_inc(s_x_out[i], 16)

            load_x(0)
            with sp.Fori(0, batches - 1) as b:
                stack(b)
                sp.wait_ge(s_scores, b * SCORED + SCORED)
                load_x(b + 1)
                store(b)
            stack(batches - 1)
            store(batches - 1)
            for i in range(4):
                sp.wait_ge(s_x_out[i], batches * 16)

        @block.gpsimd
        def _(pool):
            pool.sem_inc(s_ot, 1)
            nc.gpsimd.memset(EB[:, :, :], 0.0).then_inc(s_eb0, 1)
            pool.wait_ge(s_const, 12 * 16)
            pool.wait_ge(s_eb, TPB * 16)
            with pool.Fori(0, batches) as b:
                with pool.If(b):
                    for i in range(4):
                        pool.wait_ge(s_x_out[i], b * 16)
                    settle(pool)
                for i in range(4):
                    part = slice(i * T // 4, (i + 1) * T // 4)
                    pool.wait_ge(s_x_in[i], b * 16 + 16)
                    nc.gpsimd.tensor_tensor(X[:, part, :], XN[:, part, :],
                                            BO0[:, :].unsqueeze(1).to_broadcast([P, T // 4, C]), ALU.add).then_inc(s_bias, 1)
                pool.wait_ge(s_pick, b * 16 + 16)
                settle(pool)
                nc.gpsimd.tensor_copy(PICK, PICKF).then_inc(s_picked, 1)
                pool.wait_ge(s_flag, b + 1)
                settle(pool)
                general = pool.value_load(FLAG[0:1, 0:1], min_val=0, max_val=1)
                def normalise(after, place):
                    pool.wait_ge(s_rec, after + 1)
                    pool.wait_ge(s_pvc, after + 1)
                    nc.gpsimd.tensor_tensor(QH[:, bass.ts(place, CH)], PVC[:, :], REC[:, :], ALU.mult).then_inc(s_ot, 1)

                def maxima(c):
                    pool.wait_ge(s_gmax, b * GEN + c * STEPS + (STEPS + 1))
                    settle(pool)
                    rm = RM[:, :, :].rearrange("p h n -> p (h n)")
                    nc.gpsimd.partition_all_reduce(rm, rm, P, bass.bass_isa.ReduceOp.max).then_inc(s_gred, 1)

                with pool.If(general):
                    for c in range(2):
                        maxima(c)
                    with pool.Fori(1, NCH) as c:
                        normalise(b * NCH + c, c)
                        maxima(c + 1)
                with pool.Else():
                    pool.sem_inc(s_gred, NCH + 1)
                    with pool.Fori(1, NCH) as c:
                        normalise(b * NCH + c, c)
                normalise(b * NCH + NCH, 0)
                for i, c in enumerate(q_order):
                    pool.wait_ge(s_q1r, b * NCH + i + 1)
                    q = QE[:, c * CH:(c + 1) * CH].rearrange("p (g d) -> p g d", d=D)
                    r = QSUM[:, c * TPB * H:(c + 1) * TPB * H].unsqueeze(2).to_broadcast([P, TPB * H, D])
                    nc.gpsimd.tensor_tensor(q, q, r, ALU.mult).then_inc(s_q1n, 1)
                for i in range(T // 2):
                    pool.wait_ge(s_zx, b * T + 2 * i + 2)
                    z = ZX[:, i % 2, :, :]
                    n = b * PAIRS + 3 * i
                    if i:
                        pool.wait_ge(s_zs, n)
                    nc.gpsimd.tensor_tensor(Z2[:, :, :], z[:, :, 0:2 * C], z[:, :, 2 * C:4 * C], ALU.add).then_inc(s_zs, 1)
                    pool.wait_ge(s_zs, n + 1)
                    nc.gpsimd.tensor_tensor(Z2[:, :, 0:C], Z2[:, :, 0:C], Z2[:, :, C:2 * C], ALU.add).then_inc(s_zs, 1)
                    pool.wait_ge(s_comb, b * COMB + (i + 1) * 2 * NDVE)
                    pool.wait_ge(s_zs, n + 2)
                    part = X[:, 2 * i:2 * i + 2, :]
                    nc.gpsimd.tensor_tensor(part, part, Z2[:, :, 0:C], ALU.add).then_inc(s_zs, 1)

        @block.scalar
        def _(act):
            act.sem_inc(s_pvc, 1)
            with act.Fori(0, batches) as b:
                act.wait_ge(s_xT, b * NCH + 1)
                nc.scalar.activation(XT[:, 0:CH], BK[0], ACT.Copy).then_inc(s_raw0, 1)
                act.wait_ge(s_gn, b + 1)
                for c in range(1, NCH, 2):
                    nc.scalar.activation(XT[:, c * CH:(c + 1) * CH], BK[c], ACT.Identity,
                                         bias=SMALL[:, 4:5], scale=SMALL[:, 3:4]).then_inc(s_xn_act, 1)
                def squared(i):
                    c = i % NCH
                    act.wait_ge(s_proj, b * (3 * NCH) + (i if i < NCH else i + NCH) + 1)
                    raw = KL if i < NCH else QL
                    nc.scalar.activation(raw[:, c * CH:(c + 1) * CH], BK[c], ACT.Copy)
                    nc.scalar.activation(BK[c], BK[c], ACT.Square,
                                         accum_out=SS[:, i // NCH, c:c + 1]).then_inc(s_sq, 1)

                for i in range(NCH):
                    squared(i)
                for c in range(NCH):
                    act.wait_ge(s_proj, b * (3 * NCH) + NCH + c + 1)
                    nc.scalar.activation(V[:, c * TPB:(c + 1) * TPB, :].rearrange("p t c -> p (t c)"), BK[c],
                                         ACT.Copy).then_inc(s_v, 1)
                for i in range(NCH, 2 * NCH):
                    squared(i)
                act.wait_ge(s_bias, b * 4 + 4)
                for u in range(ACT_UNITS):
                    act.wait_ge(s_stack, b * (UNITS + H) + u + 1)
                    nc.scalar.activation(stacked(u), BK[u % 8], ACT.Copy).then_inc(s_ks_act, 1)
                act.wait_ge(s_kn, b + 1)
                nc.scalar.activation(QPH[:, CH:N], QL[:, CH:N], ACT.Copy,
                                     scale=SMALL[:, 7:8]).then_inc(s_qh, 1)
                for h in range(H // 2):
                    act.wait_ge(s_stack, b * (UNITS + H) + UNITS + h + 1)
                    nc.scalar.activation(QS[:, 0, h, :], BK[h], ACT.Copy).then_inc(s_ks_act, 1)

                def copy_out(after):
                    act.wait_ge(s_pv, after * T + RING // 2)
                    act.wait_ge(s_ot, after)
                    nc.scalar.activation(PVC[:, :], PV, ACT.Copy).then_inc(s_pvc, 1)

                def exponentials(c, first):
                    for s in range(STEPS):
                        jt, p = s // 2, s % 2
                        if s == 2 and first is None:
                            copy_out(b * NCH + c)
                        elif s == 2:
                            with act.If(first):
                                copy_out(b * NCH + c)
                        if p == 0:
                            act.wait_ge(s_pv, b * (NCH * T) + c * T + jt + 1)
                            act.wait_ge(s_adds, b * (NCH * ADDS) + c * ADDS + ADDS0 + adds_until(jt - RING // 2))
                        act.wait_ge(s_scores, b * SCORED + c * STEPS + (s + 1))
                        nc.scalar.activation(E[:, s % RING, :], S[buffer(s)].rearrange("p a n -> p (a n)"), ACT.Exp,
                                             scale=SCALE0).then_inc(s_exp, 1)

                with act.Fori(0, NCH // 2) as two:
                    exponentials(two * 2, two)
                    exponentials(two * 2 + 1, None)
                copy_out(b * NCH + NCH)
                def normed(done, half):
                    act.wait_ge(s_ln, b * 4 + 2 * done + half + 1)
                    chunks = range(half * HCH, (half + 1) * HCH)
                    for c in chunks[1::2]:
                        for t in range(c * TPB, (c + 1) * TPB):
                            last = nc.scalar.activation(QL[:, t * C:(t + 1) * C], X[:, t, :], ACT.Identity,
                                                        bias=NM[:, t:t + 1], scale=RY[:, t:t + 1])
                        last.then_inc(s_z_a, 1)
                    for c in chunks:
                        act.wait_ge(s_zT, b * (2 * NCH) + done * NCH + c + 1)
                        nc.scalar.activation(XT[:, c * CH:(c + 1) * CH], BK[c], ACT.Copy).then_inc(s_zc, 1)

                def keys(c):
                    act.wait_ge(s_k1, b * NCH + c + 1)
                    nc.scalar.activation(KH[:, c * CH:(c + 1) * CH], BK[c], ACT.Copy).then_inc(s_k1c, 1)

                def values1(c):
                    act.wait_ge(s_v1, b * NCH + c + 1)
                    nc.scalar.activation(V[:, c * TPB:(c + 1) * TPB, :].rearrange("p t c -> p (t c)"), BK[c],
                                         ACT.Copy).then_inc(s_v1c, 1)

                for half in range(2):
                    chunks = range(half * HCH, (half + 1) * HCH)
                    normed(0, half)
                    for c in chunks:
                        keys(c)
                    if half == 0:
                        for c in chunks:
                            values1(c)
                def q_exponentials(chunks):
                    for c in chunks:
                        act.wait_ge(s_q1s, b * NCH + c + 1)
                        nc.scalar.activation(QE[:, c * CH:(c + 1) * CH], QE[:, c * CH:(c + 1) * CH],
                                             ACT.Exp).then_inc(s_q1e, 1)

                q_exponentials(range(HCH // 2))
                act.wait_ge(s_k1x, b + 1)
                for half in (1, 0):
                    kh = KH[:, half * HALF * P:(half + 1) * HALF * P]
                    nc.scalar.activation(kh, kh, ACT.Exp, bias=SMALL[:, 8:9],
                                         accum_out=KSUM[:, half:half + 1]).then_inc(s_k1e, 1)
                for c in range(HCH, NCH):
                    values1(c)
                q_exponentials(range(HCH // 2, HCH))
                for i, c in enumerate(k_order):
                    act.wait_ge(s_kT, b * NCH + i + 1)
                    nc.scalar.activation(KL[:, c * CH:(c + 1) * CH], BK[c], ACT.Copy).then_inc(s_kTc, 1)
                q_exponentials(range(HCH, NCH))
                for i, c in enumerate(q_order):
                    act.wait_ge(s_qT, b * NCH + i + 1)
                    nc.scalar.activation(QT[:, c * CH:(c + 1) * CH], BK[c], ACT.Copy).then_inc(s_qTc, 1)
                normed(1, 0)
                normed(1, 1)
                for half in range(2):
                    pr = PR[:, half * HALF:(half + 1) * HALF, :]
                    act.wait_ge(s_rt, b * 2 + half + 1)
                    nc.scalar.activation(pr, pr, ACT.Exp).then_inc(s_rte, 1)
                for t in range(T):
                    if t % HALF == 0:
                        act.wait_ge(s_gate, b * 2 + t // HALF + 1)
                    if t % 2 == 0 and t >= 4:
                        act.wait_ge(s_zs, b * PAIRS + 3 * (t // 2 - 2) + 1)
                    act.wait_ge(s_ex, b * T + t + 1)
                    for e in range(NDVE, EXPERTS):
                        k = slice((e - NDVE) * C, (e - NDVE + 1) * C)
                        last = nc.scalar.activation(ZX[:, t // 2 % 2, t % 2, k], expert_bank(t, 1)[:, k], ACT.Copy,
                                                    scale=GT[:, t, e:e + 1])
                    last.then_inc(s_zx, 1)

        @block.vector
        def _(dve):
            v = nc.vector

            def chain(done, before):
                n = [0]

                def link(instruction):
                    n[0] += 1
                    instruction.then_inc(done, 1)
                    dve.wait_ge(done, before + n[0])

                return link, n

            def rsqrt(link, y, a, n):
                t, u = RT[:, 0:n], RU[:, 0:n]
                link(v.tensor_scalar(t.bitcast(U32), a.bitcast(U32), 1, None, ALU.logical_shift_right))
                link(v.tensor_scalar(y.bitcast(I32), t.bitcast(I32), -1.0, float(MAGIC), ALU.mult, ALU.add))
                for _ in range(3):
                    link(v.tensor_tensor(u, y, y, ALU.mult))
                    link(v.scalar_tensor_tensor(u, u, -0.5, a, ALU.mult, ALU.mult))
                    link(v.scalar_tensor_tensor(y, u, 1.5, y, ALU.add, ALU.mult))

            def statistics(c):
                for t in range(c * TPB, (c + 1) * TPB):
                    last = v.bn_stats(ST[:, t, :], X[:, t, :])
                return last

            def layernorm(mix_link, half, last):
                mix_link(last)
                tiles = slice(half * HALF, (half + 1) * HALF)
                me, qe, mo, qo = (ST[:, tiles, i] for i in (1, 2, 4, 5))
                mean, ra, rt, ru = MEAN[:, tiles], RA[:, 0:HALF], RT[:, 0:HALF], RU[:, 0:HALF]
                v.tensor_tensor(mean, me, mo, ALU.add)
                v.tensor_tensor(ru, qe, qo, ALU.add)
                mix_link(v.tensor_tensor(ra, me, mo, ALU.subtract))
                v.tensor_scalar(mean, mean, 0.5, None, ALU.mult)
                v.tensor_scalar(ru, ru, 1.0 / C, 1e-5, ALU.mult, ALU.add)
                mix_link(v.tensor_tensor(rt, ra, ra, ALU.mult))
                mix_link(v.scalar_tensor_tensor(ra, rt, 0.25, ru, ALU.mult, ALU.add))
                rsqrt(mix_link, RY[:, tiles], ra, HALF)
                v.scalar_tensor_tensor(NM[:, tiles], mean, -1.0, RY[:, tiles], ALU.mult, ALU.mult).then_inc(s_ln, 1)
                for c in range(half * HCH, (half + 1) * HCH, 2):
                    for t in range(c * TPB, (c + 1) * TPB):
                        last = v.tensor_scalar(QL[:, t * C:(t + 1) * C], X[:, t, :], MEAN[:, t:t + 1], RY[:, t:t + 1],
                                               ALU.subtract, ALU.mult)
                    last.then_inc(s_z_d, 1)

            dve.sem_inc(s_adds, ADDS0)
            dve.sem_inc(s_rec, 1)
            dve.sem_inc(s_gmax, 1)
            dve.wait_ge(s_const, 12 * 16)
            with dve.Fori(0, batches) as b:
                pre_link, pre_n = chain(s_pre, b * PRE_LINKS)
                for c in (*range(1, NCH), 0):
                    if c:
                        dve.wait_ge(s_xT, b * NCH + c + 1)
                    else:
                        dve.wait_ge(s_raw0, b + 1)
                    last = v.bn_stats(ST[:, c, :], BK[c])
                pre_link(last)
                settle(dve)
                v.bn_aggr(MV[:, :], ST[:, 0:NCH, :].rearrange("p a s -> p (a s)")).then_inc(s_cst, 1)
                dve.wait_ge(s_gm, b * 3 + 1)
                pre_link(v.tensor_copy(SMALL[:, 0:1], BK[0][:, 0:1]))
                pre_link(v.tensor_tensor(SMALL[:, 1:2], MV[:, 0:1], SMALL[:, 0:1], ALU.subtract))
                v.scalar_tensor_tensor(SMALL[:, 2:3], SMALL[:, 1:2], SMALL[:, 1:2], MV[:, 1:2],
                                       ALU.mult, ALU.add).then_inc(s_cst, 1)
                dve.wait_ge(s_gm, b * 3 + 2)
                pre_link(v.tensor_scalar(RA[:, 0:1], BK[0][:, 1:2], 1e-5, None, ALU.add))
                rsqrt(pre_link, SMALL[:, 3:4], RA[:, 0:1], 1)
                v.scalar_tensor_tensor(SMALL[:, 4:5], SMALL[:, 0:1], -1.0, SMALL[:, 3:4],
                                       ALU.mult, ALU.mult).then_inc(s_gn, 1)
                for c in range(0, NCH, 2):
                    v.tensor_scalar(XT[:, c * CH:(c + 1) * CH], XT[:, 0:CH] if c == 0 else BK[c],
                                    SMALL[:, 0:1], SMALL[:, 3:4], ALU.subtract, ALU.mult).then_inc(s_xn_dve, 1)

                for m in range(2):
                    for c in range(NCH):
                        dve.wait_ge(s_sq, b * (2 * NCH) + m * NCH + c + 1)
                        v.reduce_max(MXS[:, m, c:c + 1], BK[c], X_AX).then_inc(s_sqmax, 1)
                    pre_link(v.reduce_sum(RA[:, 1:2], SS[:, m, :], X_AX))
                    pre_link(v.tensor_scalar(RA[:, 0:1], RA[:, 1:2], 1e-24, None, ALU.max))
                    rsqrt(pre_link, SMALL[:, 6 + m:7 + m], RA[:, 0:1], 1)
                    if m == 0:
                        v.tensor_scalar(KPH, KL, SMALL[:, 6:7], None, ALU.mult).then_inc(s_kh, 1)
                        dve.wait_ge(s_kh, b * 5 + 1)
                        for half in range(2):
                            part = slice(half * N // 2, (half + 1) * N // 2)
                            v.scalar_tensor_tensor(KPL[:, part], KL[:, part], SMALL[:, 6:7], KPH[:, part].bitcast(F32),
                                                   ALU.mult, ALU.subtract).then_inc(s_kh, 1)
                    else:
                        dve.wait_ge(s_sqmax, b * (2 * NCH) + 2 * NCH)
                        pre_link(v.reduce_max(SMALL[:, 10:12], MXS[:, :, :], X_AX))
                        pre_link(v.tensor_tensor(SMALL[:, 12:14], SMALL[:, 6:8], SMALL[:, 6:8], ALU.mult))
                        pre_link(v.tensor_tensor(SMALL[:, 12:14], SMALL[:, 12:14], SMALL[:, 10:12], ALU.mult))
                        v.reduce_sum(SMALL[:, 14:15], SMALL[:, 12:14], X_AX).then_inc(s_kn, 1)
                        first, others = slice(0, CH), slice(CH, N)
                        pre_link(v.tensor_scalar(QPH[:, first], QL[:, first], SMALL[:, 7:8], None, ALU.mult))
                        v.scalar_tensor_tensor(QPL[:, first], QL[:, first], SMALL[:, 7:8], QPH[:, first].bitcast(F32),
                                               ALU.mult, ALU.subtract).then_inc(s_kh, 1)
                dve.wait_ge(s_bias, b * 4 + 4)
                for u in range(ACT_UNITS, UNITS):
                    dve.wait_ge(s_stack, b * (UNITS + H) + u + 1)
                    v.tensor_copy(stacked(u), BK[u % 8]).then_inc(s_ks_dve, 1)
                for h in range(H // 2, H):
                    dve.wait_ge(s_stack, b * (UNITS + H) + UNITS + h + 1)
                    v.tensor_copy(QS[:, 0, h, :], BK[h]).then_inc(s_ks_dve, 1)
                dve.wait_ge(s_gm, b * 3 + 3)
                v.tensor_scalar(FLAG[:, :], BK[4][:, 0:1], 2.0 * safe_bound / SCALE0, None,
                                ALU.is_gt).then_inc(s_flag, 1)
                dve.wait_ge(s_qh, b + 1)
                v.scalar_tensor_tensor(QPL[:, others], QL[:, others], SMALL[:, 7:8],
                                       QPH[:, others].bitcast(F32), ALU.mult, ALU.subtract).then_inc(s_kh, 1)
                dve.wait_ge(s_flag, b + 1)
                assert pre_n[0] == PRE_LINKS, pre_n

                def maxima(first):
                    for s in range(STEPS):
                        jt, p = s // 2, s % 2
                        dve.wait_ge(s_gscore, first + (s + 1))
                        rm = RM[:, 2 * p:2 * p + 2, :]
                        if jt == 0:
                            v.tensor_copy(rm, GS).then_inc(s_gmax, 1)
                        else:
                            dve.wait_ge(s_gmax, first + s)
                            v.tensor_tensor(rm, GS, rm, ALU.max).then_inc(s_gmax, 1)

                def attend(two, par, safe):
                    c = two * 2 + par
                    chunk = b * NCH + c
                    for g in range(NG):
                        for jt in range(FIRST[g] + 1, END[g]):
                            if jt == NORMALISED:
                                if par:
                                    reciprocals(chunk)
                                else:
                                    with dve.If(two):
                                        reciprocals(chunk)
                            for p in range(2):
                                acc = ACC[:, (par * NG + g) % 2, p, :]
                                if jt == FIRST[g] + 1:
                                    if p == 0:
                                        dve.wait_ge(s_sum, chunk * NG + g + 1)
                                    one = E[:, (2 * jt - 2 + p) % RING, :]
                                else:
                                    one = acc
                                    dve.wait_ge(s_adds, chunk * ADDS + ADDS0 + 2 * (jt - g - 1) + p - 1)
                                dve.wait_ge(s_exp, chunk * STEPS + 2 * jt + p + 1)
                                v.tensor_tensor(acc, one, E[:, (2 * jt + p) % RING, :], ALU.add).then_inc(s_adds, 1)
                    if not safe:
                        maxima(b * GEN + c * STEPS + STEPS)

                def reciprocals(after):
                    dve.wait_ge(s_sum, after * NG + 2)
                    dve.wait_ge(s_ot, after)
                    v.reciprocal(REC[:, :], SM).then_inc(s_rec, 1)

                settle(dve)
                general = dve.value_load(FLAG[0:1, 0:1], min_val=0, max_val=1)
                with dve.If(general):
                    maxima(b * GEN)
                    with dve.Fori(0, NCH // 2) as two:
                        attend(two, 0, False)
                        attend(two, 1, False)
                with dve.Else():
                    dve.sem_inc(s_gmax, GEN)
                    with dve.Fori(0, NCH // 2) as two:
                        attend(two, 0, True)
                        attend(two, 1, True)

                mix_link, mix_n = chain(s_mix, b * MIX_LINKS)
                dve.wait_ge(s_bias, b * 4 + 4)

                def onto_x(ready, done, c):
                    dve.wait_ge(ready, b * NCH + c + 1)
                    part = X[:, c * TPB:(c + 1) * TPB, :].rearrange("p t c -> p (t c)")
                    v.tensor_tensor(part, BK[c], part, ALU.add).then_inc(done, 1)

                def onto_x_and_normed(ready, done, half):
                    first = half * HCH
                    for c in range(first, first + HCH):
                        onto_x(ready, done, c)
                        if c > first:
                            dve.wait_ge(done, b * NCH + c)
                            statistics(c - 1)
                    dve.wait_ge(done, b * NCH + first + HCH)
                    layernorm(mix_link, half, statistics(first + HCH - 1))

                onto_x_and_normed(s_y0, s_x0, 0)
                reciprocals(b * NCH + NCH)
                onto_x_and_normed(s_y0, s_x0, 1)

                def k_maxima(chunks):
                    for c in chunks:
                        dve.wait_ge(s_k1c, b * NCH + c + 1)
                        v.reduce_max(MXS[:, 0, c:c + 1], KH[:, c * CH:(c + 1) * CH], X_AX).then_inc(s_k1m, 1)

                def q_shifted(chunks):
                    for c in chunks:
                        g = slice(c * TPB * H, (c + 1) * TPB * H)
                        dve.wait_ge(s_q1, b * NCH + c + 1)
                        q = BK[c].rearrange("p (g d) -> p g d", d=D)
                        e = QE[:, c * CH:(c + 1) * CH].rearrange("p (g d) -> p g d", d=D)
                        mix_link(v.reduce_max(QM[:, g], q, X_AX))
                        v.tensor_tensor(e, q, QM[:, g].unsqueeze(2).to_broadcast([P, TPB * H, D]),
                                        ALU.subtract).then_inc(s_q1s, 1)

                def q_summed(places):
                    for c in q_order[places]:
                        g = slice(c * TPB * H, (c + 1) * TPB * H)
                        dve.wait_ge(s_q1e, b * NCH + c + 1)
                        mix_link(v.reduce_sum(QSUM[:, g], QE[:, c * CH:(c + 1) * CH].rearrange("p (g d) -> p g d", d=D), X_AX))
                        v.reciprocal(QSUM[:, g], QSUM[:, g]).then_inc(s_q1r, 1)

                k_maxima(range(HCH))
                q_shifted(range(HCH // 2))
                k_maxima(range(HCH, NCH))
                dve.wait_ge(s_k1m, b * NCH + NCH)
                mix_link(v.reduce_max(SMALL[:, 10:11], MXS[:, 0, :], X_AX))
                v.tensor_scalar(SMALL[:, 8:9], SMALL[:, 10:11], -1.0, None, ALU.mult).then_inc(s_k1x, 1)
                q_shifted(range(HCH // 2, HCH))
                q_summed(slice(0, HCH - 1))
                q_shifted(range(HCH, NCH))
                q_summed(slice(HCH - 1, HCH))
                dve.wait_ge(s_k1e, b * 2 + 2)
                mix_link(v.tensor_tensor(SMALL[:, 9:10], KSUM[:, 0:1], KSUM[:, 1:2], ALU.add))
                mix_link(v.reciprocal(SMALL[:, 11:12], SMALL[:, 9:10]))
                dve.wait_ge(s_ctx, b * 2 + 1)
                v.scalar_tensor_tensor(CTX[:, :], BK[0][:, 0:C], SMALL[:, 11:12], BLOCK,
                                       ALU.mult, ALU.mult).then_inc(s_at, 1)
                q_summed(slice(HCH, NCH))
                dve.wait_ge(s_ctx, b * 2 + 2)
                v.scalar_tensor_tensor(AT[:, :], BO1[:, :], 1.0 / H, BK[0][:, C:2 * C],
                                       ALU.mult, ALU.add).then_inc(s_at, 1)
                mix_link(v.memset(G32[:, :, :], 0.0))
                for i, c in enumerate(q_order):
                    dve.wait_ge(s_y1, b * NCH + i + 1)
                    last = v.bn_stats(ST[:, c, :], BK[c])
                mix_link(last)
                settle(dve)
                v.bn_aggr(MV[:, :], ST[:, 0:NCH, :].rearrange("p a s -> p (a s)")).then_inc(s_bst, 1)
                dve.wait_ge(s_gst, b * 2 + 1)
                mix_link(v.tensor_copy(SMALL[:, 0:1], BK[0][:, 0:1]))
                mix_link(v.tensor_tensor(SMALL[:, 1:2], MV[:, 0:1], SMALL[:, 0:1], ALU.add))
                v.scalar_tensor_tensor(SMALL[:, 2:3], SMALL[:, 1:2], SMALL[:, 1:2], MV[:, 1:2],
                                       ALU.mult, ALU.add).then_inc(s_bst, 1)
                dve.wait_ge(s_gst, b * 2 + 2)
                mix_link(v.tensor_scalar(RA[:, 0:1], BK[0][:, 1:2], -1.0, 1e-5, ALU.mult, ALU.add))
                rsqrt(mix_link, SMALL[:, 3:4], RA[:, 0:1], 1)
                mix_link(v.tensor_scalar(GA[:, :], GNW[:, :], SMALL[:, 3:4], None, ALU.mult))
                v.scalar_tensor_tensor(GB[:, :], GA[:, :], SMALL[:, 0:1], GNB[:, :], ALU.mult, ALU.add)
                mix_link(v.tensor_tensor(AT2[:, :], AT[:, :], GA[:, :], ALU.mult))
                v.scalar_tensor_tensor(AT2[:, :], GB[:, :], 1.0 / H, AT2[:, :], ALU.mult, ALU.add).then_inc(s_at, 1)

                for half in range(2):
                    onto_x_and_normed(s_y2, s_x1, half)

                def over(x2):
                    return x2.unsqueeze(2).to_broadcast([P, HALF, EXPERTS])

                def rows(x3, half):
                    return x3[:, half * HALF:(half + 1) * HALF]

                def logits(half):
                    l = rows(L, half)
                    bank = BK[7 * half][:, 0:HALF * EXPERTS].rearrange("p (t e) -> p t e", e=EXPERTS)
                    dve.wait_ge(s_route, b * 2 + half + 1)
                    mix_link(v.tensor_tensor(l, bank, RB[:, :].unsqueeze(1).to_broadcast([P, HALF, EXPERTS]), ALU.add))
                    mix_link(v.reduce_max(rows(R1[:, 0, :], half), l, X_AX))
                    v.tensor_tensor(rows(PR, half), l, over(rows(R1[:, 0, :], half)), ALU.subtract).then_inc(s_rt, 1)

                rank = RANK.unsqueeze(1).to_broadcast([P, HALF, EXPERTS])

                def probabilities(half):
                    pr, total = rows(PR, half), rows(R1[:, 1, :], half)
                    dve.wait_ge(s_rte, b * 2 + half + 1)
                    mix_link(v.reduce_sum(total, pr, X_AX))
                    mix_link(v.reciprocal(total, total))
                    mix_link(v.tensor_tensor(pr, pr, over(total), ALU.mult))

                def pick(half, best, onehot):
                    pr, top, best, onehot = (rows(x, half) for x in (PR, R1[:, 0, :], R1[:, best, :], onehot))
                    mix_link(v.reduce_max(best, pr, X_AX))
                    mix_link(v.tensor_tensor(onehot, pr, over(best), ALU.is_equal))
                    mix_link(v.tensor_tensor(onehot, onehot, rank, ALU.mult))
                    mix_link(v.reduce_max(top, onehot, X_AX))
                    mix_link(v.tensor_tensor(onehot, rank, over(top), ALU.is_equal))

                def second(half):
                    pr = rows(PR, half)
                    mix_link(v.scalar_tensor_tensor(pr, rows(OH, half), -2.0, pr, ALU.mult, ALU.add))
                    pick(half, 3, TK)

                def gates(half):
                    total, p1, p2 = (rows(R1[:, i, :], half) for i in (1, 2, 3))
                    oh, tk = rows(OH, half), rows(TK, half)
                    mix_link(v.tensor_tensor(total, p1, p2, ALU.add))
                    mix_link(v.reciprocal(total, total))
                    v.tensor_tensor(p1, p1, total, ALU.mult)
                    mix_link(v.tensor_tensor(p2, p2, total, ALU.mult))
                    v.tensor_tensor(oh, oh, over(p1), ALU.mult)
                    mix_link(v.tensor_tensor(tk, tk, over(p2), ALU.mult))
                    v.tensor_tensor(rows(GT, half), oh, tk, ALU.add)
                    v.tensor_tensor(rows(G32, half)[:, :, 0:EXPERTS], oh, tk, ALU.add).then_inc(s_gate, 1)

                def gates_out(half):
                    dve.wait_ge(s_gtT, b * 2 + half + 1)
                    v.tensor_copy(GTT[:, HCH * half:HCH * (half + 1), :].rearrange("p a n -> p (a n)"),
                                  BK[7 * half]).then_inc(s_gtc, 1)

                def combine(c):
                    part = X[:, c * TPB:(c + 1) * TPB, :].rearrange("p t c -> p (t c)")
                    dve.wait_ge(s_ebm, b * NCH + c + 1)
                    v.tensor_tensor(part, BK[7 * (c // HCH)], part, ALU.add).then_inc(s_eba, 1)
                    dve.wait_ge(s_eba, b * NCH + c + 1)
                    for t in range(c * TPB, (c + 1) * TPB):
                        dve.wait_ge(s_ex, b * T + t + 1)
                        for e in range(NDVE):
                            if e:
                                dve.wait_ge(s_comb, b * COMB + t * NDVE + e)
                            v.scalar_tensor_tensor(X[:, t, :], expert_bank(t, 0)[:, e * C:(e + 1) * C],
                                                   GT[:, t, e:e + 1], X[:, t, :], ALU.mult, ALU.add).then_inc(s_comb, 1)

                logits(0)
                probabilities(0)
                pick(0, 2, OH)
                second(0)
                gates(0)
                logits(1)
                gates_out(0)
                combine(0)
                probabilities(1)
                pick(1, 2, OH)
                combine(1)
                second(1)
                combine(2)
                gates(1)
                gates_out(1)
                combine(3)
                for c in range(HCH, NCH):
                    combine(c)
                assert mix_n[0] == MIX_LINKS, mix_n

        @block.tensor
        def _(pe):
            def mm(o, lhsT, rhs, start=True, stop=True, shared=False):
                return nc.tensor.matmul(o, lhsT, rhs, start=start, stop=stop, skip_group_check=shared)

            def transposes(dst, src, c):
                for t in range(c * TPB, (c + 1) * TPB):
                    last = nc.tensor.transpose(dst[:, (t % TPB) * P:(t % TPB + 1) * P], src(t), IDENT)
                return last

            pe.sem_inc(s_pv, RING // 2)
            pe.sem_inc(s_sum, 2)
            pe.wait_ge(s_const, 12 * 16)
            pe.wait_ge(s_eb, TPB * 16)
            with pe.Fori(0, batches) as b:
                with pe.If(b):
                    pe.wait_ge(s_comb, b * COMB)
                    pe.wait_ge(s_zx, b * T)
                    settle(pe)
                for c in range(NCH):
                    if c % 2 == 0:
                        pe.wait_ge(s_x_in[c // 2], b * 16 + 16)
                    transposes(BK[c], lambda t: XN[:, t, :], c).then_inc(s_xT, 1)
                pe.wait_ge(s_raw0, b + 1)
                pe.wait_ge(s_cst, b * 2 + 1)
                mm(BK[0][:, 0:1], GAVG, MV[:, 0:1]).then_inc(s_gm, 1)
                pe.wait_ge(s_cst, b * 2 + 2)
                mm(BK[0][:, 1:2], GAVG, SMALL[:, 2:3]).then_inc(s_gm, 1)
                def projected(c, m):
                    mm(BK[c], WQKV[:, m * C:(m + 1) * C], XT[:, c * CH:(c + 1) * CH]).then_inc(s_proj, 1)

                for c in range(NCH):
                    if c % 2:
                        pe.wait_ge(s_xn_act, b * 4 + (c + 1) // 2)
                    else:
                        pe.wait_ge(s_xn_dve, b * 4 + c // 2 + 1)
                    projected(c, 1)
                for c in range(NCH):
                    pe.wait_ge(s_sqmax, b * (2 * NCH) + c + 1)
                    for t in range(c * TPB, (c + 1) * TPB):
                        last = mm(BK[c][:, (t % TPB) * C:(t % TPB + 1) * C], XT[:, t * P:(t + 1) * P], WQKV[:, 2 * C:3 * C])
                    last.then_inc(s_proj, 1)
                for c in range(NCH):
                    pe.wait_ge(s_v, b * NCH + c + 1)
                    projected(c, 0)

                def stack(bank, h, high, low, c, first):
                    for i, parts in enumerate((high, low)):
                        k = (first + i) * H + h
                        last = mm(bank, PICK[:, k * P:(k + 1) * P], parts[:, c * CH:(c + 1) * CH],
                                  start=(i == 0), stop=(i == 1))
                    last.then_inc(s_stack, 1)

                pe.wait_ge(s_picked, b + 1)
                for u in range(UNITS):
                    c, h = u // H, u % H
                    if h == 0 and c % HCH == 0:
                        pe.wait_ge(s_kh, b * 5 + 2 + c // HCH)
                    if u < 8:
                        pe.wait_ge(s_sqmax, b * (2 * NCH) + NCH + u + 1)
                    elif u - 8 < ACT_UNITS:
                        pe.wait_ge(s_ks_act, b * KS_ACT + u - 8 + 1)
                    else:
                        pe.wait_ge(s_ks_dve, b * KS_DVE + u - 8 - ACT_UNITS + 1)
                    stack(BK[u % 8], h, KPH, KPL, c, 0)
                pe.wait_ge(s_kh, b * 5 + 4)
                for h in range(H):
                    pe.wait_ge(s_ks_dve, b * KS_DVE + UNITS - 8 + h - ACT_UNITS + 1)
                    stack(BK[h], h, QPH, QPL, 0, 2)
                pe.wait_ge(s_kn, b + 1)
                pe.wait_ge(s_ks_dve, b * KS_DVE + UNITS - ACT_UNITS)
                mm(BK[4][:, 0:1], ONES, SMALL[:, 14:15]).then_inc(s_gm, 1)
                pe.wait_ge(s_flag, b + 1)

                def scores(s, par, safe):
                    jt, p = s // 2, s % 2
                    for i in range(2):
                        h = 2 * p + i
                        last = mm(S[buffer(s)][:, i, :], KS[:, h, jt * P:(jt + 1) * P],
                                  QS[:, par, h, :], stop=safe)
                        if not safe:
                            last = mm(S[buffer(s)][:, i, :], NEG, RM[:, h, :], start=False)
                    return last

                def maxima(par, first, reds):
                    for s in range(STEPS):
                        jt, p = s // 2, s % 2
                        pe.wait_ge(s_gmax, first + (s + 1))
                        for i in range(2):
                            last = mm(GS[:, i, :], KS[:, 2 * p + i, jt * P:(jt + 1) * P], QS[:, par, 2 * p + i, :])
                        last.then_inc(s_gscore, 1)
                    pe.wait_ge(s_gred, reds)

                def values(jt):
                    for h in range(H):
                        e = E[:, (2 * jt + h // 2) % RING, (h % 2) * CH:(h % 2 + 1) * CH]
                        last = mm(PV[D * h:D * h + D, :], V[:, jt, D * h:D * h + D], e, start=(jt == 0), stop=(jt == T - 1))
                    last.then_inc(s_pv, 1)

                def sums(g, adds, par):
                    pe.wait_ge(s_adds, adds)
                    for h in range(H):
                        a = ACC[:, (par * NG + g) % 2, h // 2, (h % 2) * CH:(h % 2 + 1) * CH]
                        last = mm(SM[D * h:D * h + D, :], ONES[:, 0:D], a, start=(g == 0), stop=(g == NG - 1))
                    last.then_inc(s_sum, 1)

                def attend(two, par, safe):
                    c = two * 2 + par
                    chunk = b * NCH + c
                    for s in range(STEPS):
                        jt = s // 2
                        pe.wait_ge(s_exp, chunk * STEPS + s + 1)
                        for t in scored_after(s):
                            if t == STEPS:
                                pe.wait_ge(s_q_in, b * QLOADS + (c + 2) * 256)
                                if not safe:
                                    maxima(1 - par, b * GEN + c * STEPS + STEPS, b * (NCH + 1) + c + 2)
                            scores(t % STEPS, par if t < STEPS else 1 - par, safe).then_inc(s_scores, 1)
                        if s % 2:
                            if jt == 0:
                                pe.wait_ge(s_pvc, chunk + 1)
                            values(jt)
                            if jt == LAG - 1:
                                if par:
                                    sums(NG - 1, chunk * ADDS + ADDS0, 0)
                                else:
                                    with pe.If(two):
                                        sums(NG - 1, chunk * ADDS + ADDS0, 1)
                            for g in range(NG - 1):
                                if jt == END[g] - 1 + LAG:
                                    if g == 0:
                                        pe.wait_ge(s_rec, chunk + 1)
                                    sums(g, chunk * ADDS + (ADDS0 + 2 * (END[g] - g - 1)), par)

                pe.wait_ge(s_ks_act, b * KS_ACT + KS_ACT)
                pe.wait_ge(s_ks_dve, b * KS_DVE + KS_DVE)
                settle(pe)
                general = pe.value_load(FLAG[0:1, 0:1], min_val=0, max_val=1)
                with pe.If(general):
                    maxima(0, b * GEN, b * (NCH + 1) + 1)
                    for s in range(AHEAD):
                        scores(s, 0, False).then_inc(s_scores, 1)
                    with pe.Fori(0, NCH // 2) as two:
                        attend(two, 0, False)
                        attend(two, 1, False)
                with pe.Else():
                    pe.sem_inc(s_gscore, GEN)
                    for s in range(AHEAD):
                        scores(s, 0, True).then_inc(s_scores, 1)
                    with pe.Fori(0, NCH // 2) as two:
                        attend(two, 0, True)
                        attend(two, 1, True)

                def tiles(lhsT, rhs, signal, before=None, onto=None):
                    for c in range(NCH):
                        if before:
                            before(c)
                        for t in range(c * TPB, (c + 1) * TPB):
                            last = mm(BK[c][:, (t % TPB) * C:(t % TPB + 1) * C], lhsT(t), rhs(t))
                        last.then_inc(signal, 1)

                def project(c):
                    for t in range(c * TPB, (c + 1) * TPB):
                        place = (t + TPB) % T
                        last = mm(BK[c][:, (t % TPB) * C:(t % TPB + 1) * C], QH[:, place * P:(place + 1) * P], WOUT0[:, :])
                    last.then_inc(s_y0, 1)

                pe.wait_ge(s_ot, b * NCH + NCH)
                for c in range(3):
                    project(c)
                project(3)
                sums(NG - 1, (b * NCH + NCH) * ADDS + ADDS0, 1)
                project(4)
                project(5)
                pe.wait_ge(s_pvc, b * NCH + NCH + 1)
                project(6)

                def transposed(done, c):
                    if c % 2:
                        pe.wait_ge(s_z_a, b * NCH + done * (NCH // 2) + c // 2 + 1)
                    else:
                        pe.wait_ge(s_z_d, b * NCH + done * (NCH // 2) + c // 2 + 1)
                    transposes(BK[c], lambda t: QL[:, t * C:(t + 1) * C], c).then_inc(s_zT, 1)

                def token_major(c, weights, signal):
                    for t in range(c * TPB, (c + 1) * TPB):
                        last = mm(BK[c][:, (t % TPB) * C:(t % TPB + 1) * C], XT[:, t * P:(t + 1) * P], weights)
                    last.then_inc(signal, 1)

                for half in range(2):
                    chunks = range(half * HCH, (half + 1) * HCH)
                    for c in chunks:
                        transposed(0, c)
                    for c in chunks:
                        pe.wait_ge(s_zc, b * (2 * NCH) + c + 1)
                        mm(BK[c], WQKV1[:, C:2 * C], XT[:, c * CH:(c + 1) * CH]).then_inc(s_k1, 1)
                    if half == 0:
                        pe.wait_ge(s_ot, b * NCH + NCH + 1)
                        project(7)
                    for c in chunks:
                        pe.wait_ge(s_k1c, b * NCH + c + 1)
                        token_major(c, WQKV1[:, 2 * C:3 * C], s_v1)
                    if half == 0:
                        for c in chunks:
                            pe.wait_ge(s_v1c, b * NCH + c + 1)
                            token_major(c, WQKV1[:, 0:C], s_q1)
                for i, c in enumerate(k_order):
                    if i % HCH == 0:
                        pe.wait_ge(s_k1e, b * 2 + i // HCH + 1)
                    if c >= HCH:
                        pe.wait_ge(s_v1c, b * NCH + c + 1)
                    else:
                        pe.wait_ge(s_q1s, b * NCH + c + 1)
                    transposes(BK[c], lambda t: KH[:, t * P:(t + 1) * P], c).then_inc(s_kT, 1)
                for c in range(HCH, NCH):
                    pe.wait_ge(s_kTc, b * NCH + c - HCH + 1)
                    token_major(c, WQKV1[:, 0:C], s_q1)
                pe.wait_ge(s_kTc, b * NCH + NCH)
                for t in range(T):
                    last = mm(BK[0][:, 0:C], KL[:, t * P:(t + 1) * P], V[:, t, :], start=(t == 0), stop=(t == T - 1))
                last.then_inc(s_ctx, 1)
                for i, c in enumerate(q_order):
                    if i == 4:
                        pe.wait_ge(s_at, b * 3 + 1)
                        mm(BK[0][:, C:2 * C], CTX[:, :], WOUT1[:, :]).then_inc(s_ctx, 1)
                    if c == 0:
                        pe.wait_ge(s_at, b * 3 + 2)
                    pe.wait_ge(s_q1n, b * NCH + i + 1)
                    transposes(BK[c], lambda t: QE[:, t * P:(t + 1) * P], c).then_inc(s_qT, 1)
                for i, c in enumerate(q_order):
                    pe.wait_ge(s_qTc, b * NCH + i + 1)
                    for t in range(c * TPB, (c + 1) * TPB):
                        last = mm(BK[c][:, (t % TPB) * C:(t % TPB + 1) * C], QT[:, t * P:(t + 1) * P], AT[:, :])
                    last.then_inc(s_y1, 1)
                pe.wait_ge(s_bst, b * 2 + 1)
                mm(BK[0][:, 0:1], NEG, MV[:, 0:1]).then_inc(s_gst, 1)
                pe.wait_ge(s_bst, b * 2 + 2)
                mm(BK[0][:, 1:2], NEG, SMALL[:, 2:3]).then_inc(s_gst, 1)
                pe.wait_ge(s_at, b * 3 + 3)
                tiles(lambda t: QT[:, t * P:(t + 1) * P], lambda t: AT2[:, :], s_y2)

                for half in range(2):
                    for c in range(half * HCH, (half + 1) * HCH):
                        transposed(1, c)
                    pe.wait_ge(s_zc, b * (2 * NCH) + NCH + (half + 1) * HCH)
                    for i in range(HALF):
                        t = half * HALF + i
                        last = mm(BK[7 * half][:, i * EXPERTS:(i + 1) * EXPERTS], XT[:, t * P:(t + 1) * P], WR[:, :])
                    last.then_inc(s_route, 1)

                def gates(half):
                    pe.wait_ge(s_gate, b * 2 + half + 1)
                    for k in range(HCH):
                        a = HCH * half + k
                        last = nc.tensor.transpose(BK[7 * half][:, k * P:(k + 1) * P],
                                                   G32[:, TPB * a:TPB * (a + 1), :].rearrange("p t e -> p (t e)"), IDENT)
                    last.then_inc(s_gtT, 1)

                def biases(c):
                    if c % HCH == 0:
                        pe.wait_ge(s_gtc, b * 2 + c // HCH + 1)
                    else:
                        pe.wait_ge(s_eba, b * NCH + c)
                    for t in range(TPB):
                        last = mm(BK[7 * (c // HCH)][:, t * C:(t + 1) * C], GTT[:, c, :], EB[:, t, :])
                    last.then_inc(s_ebm, 1)

                for t in range(T):
                    if t == 1:
                        gates(0)
                    if t == 2:
                        biases(0)
                    if t == HALF - TPB + 1:
                        gates(1)
                    if t % TPB == 0 and t:
                        biases(t // TPB)
                    if t >= EBUF:
                        pe.wait_ge(s_comb, b * COMB + (t - EBUF + 1) * NDVE)
                        pe.wait_ge(s_zx, b * T + t - EBUF + 1)
                    for part in range(2):
                        last = mm(expert_bank(t, part), XT[:, t * P:(t + 1) * P],
                                  WEXP[:, part * NDVE:(part + 1) * NDVE, :].rearrange("p e c -> p (e c)"))
                    last.then_inc(s_ex, 1)


_INS = ["x", "L0_conv_w_qkv", "L0_conv_w_out", "L0_conv_b_out", "L1_attn_W_qkv", "L1_attn_W_out", "L1_attn_b_out",
        "L1_attn_gn_w", "L1_attn_gn_b", "L1_ffn_router_w", "L1_ffn_router_b", "L1_ffn_expert_w", "L1_ffn_expert_b"]


def constants():
    i = np.arange(P)
    per = C // G
    rank = np.zeros((P, P))
    rank[:, 0:EXPERTS] = EXPERTS - np.arange(EXPERTS)
    return np.concatenate([
        np.eye(P), (i[:, None] // per == i[None, :] // per) / per, np.ones((P, P)), np.full((P, P), -1.0 / P),
        (i[:, None] // D == i[None, :] // D) * SCALE1, rank,
        *((i[:, None] == h * D + i[None, :] % D) * np.isin(i // D, groups)
          for groups in ((0, 1), (2, 3), (0, 2), (1, 3)) for h in range(H))], axis=1).astype(np.float32)


def kernel(**inputs):
    import concourse.bacc as bacc
    from concourse.bass_utils import run_bass_kernel_spmd

    nc = bacc.Bacc("TRN2", target_bir_lowering=False, num_devices=1, dynamic_dma_scratch_size=1024)
    given = {n: np.asarray(inputs[n]) for n in _INS}
    for n in ("L1_attn_W_qkv", "L1_attn_W_out"):
        given[n] = given[n].T
    given["consts"] = constants()
    arrays, args = {}, []
    for n, a in given.items():
        arrays[f"in_{n}"] = np.ascontiguousarray(a)
        args.append(nc.dram_tensor(f"in_{n}", a.shape, mybir.dt.from_np(a.dtype), kind="ExternalInput").ap())
    args.append(nc.dram_tensor("out_0", (B, 64, 64, C), F32, kind="ExternalOutput").ap())
    hybrid_kernel(nc, *args)
    r = run_bass_kernel_spmd(nc, [arrays], core_ids=[0])
    return np.asarray(r.results[0]["out_0"])
```
